# Optimizing a Trainium2 kernel written in Bass

```python
import numpy as np
import jax
import jax.numpy as jnp

def _softmax(x, axis=-1):
    return jax.nn.softmax(x, axis=axis)

def _gelu(x):
    return jax.nn.gelu(x, approximate=True)

def _silu(x):
    return jax.nn.silu(x)

def _sigmoid(x):
    return jax.nn.sigmoid(x)

def _layernorm(x, axis=-1, eps=1e-05):
    m = jnp.mean(x, axis=axis, keepdims=True)
    v = jnp.var(x, axis=axis, keepdims=True)
    return (x - m) / jnp.sqrt(v + eps)

def _scatter_add(tgt, idx, src, axis=0):
    return tgt.at[idx].add(src)

def _segment_sum(src, seg, n):
    return jax.ops.segment_sum(src, seg, n)
kernel_name = 'mk_conv_preact_d2_conv_nchw256_r4_9e6244'

def setup_inputs(seed: int=0):
    np.random.seed(seed)
    _w = jnp.asarray

    def _rec_inputs():
        import jax
        import jax.numpy as jnp
        _gk = jax.random.key(seed)
        x = -0.000125 + 0.9999 * jax.random.normal(jax.random.fold_in(_gk, 1), (2, 64, 64, 64), jnp.float32)
        return x
    x = _rec_inputs()

    def _L0_conv_setup():
        import jax, jax.numpy as jnp
        import numpy as np
        B, N, D = (2, 64, 64)
        key = jax.random.key(seed)
        ks = jax.random.split(key, 9)
        s = 1.0 / np.sqrt(D)
        return {'pair_repr': jax.random.normal(ks[0], (B, N, N, D), dtype=jnp.float32), 'Wa': jax.random.uniform(ks[1], (D, D), jnp.float32, -s, s), 'ba': jax.random.uniform(ks[2], (D,), jnp.float32, -s, s), 'Wb': jax.random.uniform(ks[3], (D, D), jnp.float32, -s, s), 'bb': jax.random.uniform(ks[4], (D,), jnp.float32, -s, s), 'Wg': jax.random.uniform(ks[5], (D, D), jnp.float32, -s, s), 'bg': jax.random.uniform(ks[6], (D,), jnp.float32, -s, s), 'Wo': jax.random.uniform(ks[7], (D, D), jnp.float32, -s, s), 'bo': jax.random.uniform(ks[8], (D,), jnp.float32, -s, s)}
    _L0_conv_all = _L0_conv_setup()
    _L0_conv_in = {k: v for k, v in _L0_conv_all.items() if k in ('Wa', 'ba', 'Wb', 'bb', 'Wg', 'bg', 'Wo', 'bo')}
    del _L0_conv_all

    def _L1_conv_setup():
        import jax, jax.numpy as jnp
        import numpy as np
        from jax import lax
        B, C, H, W = (8, 64, 32, 32)
        KS = 4
        key = jax.random.key(seed)
        x = jax.random.normal(key, (B, C, H, W), dtype=jnp.float32)
        k1 = jnp.array([1.0, 3.0, 3.0, 1.0], dtype=jnp.float32)
        k2 = jnp.outer(k1, k1)
        k2 = k2 / k2.sum() * 4.0
        filt = jnp.broadcast_to(k2[None, None, :, :], (C, 1, KS, KS)).astype(jnp.float32)
        return {'x': x, 'filt': filt}
    _L1_conv_all = _L1_conv_setup()
    _L1_conv_in = {k: v for k, v in _L1_conv_all.items() if k in ('filt',)}
    del _L1_conv_all
    return {'x': x, 'L0_conv_Wa': _L0_conv_in['Wa'], 'L0_conv_ba': _L0_conv_in['ba'], 'L0_conv_Wb': _L0_conv_in['Wb'], 'L0_conv_bb': _L0_conv_in['bb'], 'L0_conv_Wg': _L0_conv_in['Wg'], 'L0_conv_bg': _L0_conv_in['bg'], 'L0_conv_Wo': _L0_conv_in['Wo'], 'L0_conv_bo': _L0_conv_in['bo'], 'L1_conv_filt': _L1_conv_in['filt']}

def reference(x, L0_conv_Wa, L0_conv_ba, L0_conv_Wb, L0_conv_bb, L0_conv_Wg, L0_conv_bg, L0_conv_Wo, L0_conv_bo, L1_conv_filt):
    import jax
    import jax.numpy as jnp

    def _L0_conv_ref(pair_repr, Wa, ba, Wb, bb, Wg, bg, Wo, bo):
        import jax, jax.numpy as jnp
        import numpy as np
        B, N, D = (2, 64, 64)
        a = pair_repr @ Wa + ba
        b = pair_repr @ Wb + bb
        g = jax.nn.sigmoid(pair_repr @ Wg + bg)
        ab = jnp.einsum('bijk,bikl->bijl', a, b)
        return g * ab @ Wo + bo

    def _L1_conv_ref(x, filt):
        import jax, jax.numpy as jnp
        import numpy as np
        from jax import lax
        B, C, H, W = (8, 64, 32, 32)
        KS = 4
        k = filt.shape[-1]
        c = x.shape[1]
        pad = k - 2
        p0 = (pad + 1) // 2
        p1 = pad // 2
        return lax.conv_general_dilated(x, filt, window_strides=(2, 2), padding=((p0, p1 + 1), (p0, p1 + 1)), lhs_dilation=(2, 2), dimension_numbers=('NCHW', 'OIHW', 'NCHW'), feature_group_count=c)

    def _gn(v, G=32, eps=1e-05):
        B_, C_, H_, W_ = v.shape
        g = v.reshape(B_, G, C_ // G, H_, W_)
        m = jnp.mean(g, axis=(2, 3, 4), keepdims=True)
        s = jnp.var(g, axis=(2, 3, 4), keepdims=True)
        return ((g - m) / jnp.sqrt(s + eps)).reshape(v.shape)

    def _ln_c(v, eps=1e-06):
        m = jnp.mean(v, axis=1, keepdims=True)
        s = jnp.var(v, axis=1, keepdims=True)
        return (v - m) / jnp.sqrt(s + eps)

    def _ln_t(v, eps=1e-05):
        m = jnp.mean(v, axis=-1, keepdims=True)
        s = jnp.var(v, axis=-1, keepdims=True)
        return (v - m) / jnp.sqrt(s + eps)

    def _to_tokens(v):
        B_, C_, H_, W_ = v.shape
        return v.reshape(B_, C_, H_ * W_).transpose(0, 2, 1)

    def _from_tokens(t, like):
        B_, C_, H_, W_ = like.shape
        return t.transpose(0, 2, 1).reshape(B_, C_, H_, W_)
    x = x + _L0_conv_ref(_gn(x), L0_conv_Wa, L0_conv_ba, L0_conv_Wb, L0_conv_bb, L0_conv_Wg, L0_conv_bg, L0_conv_Wo, L0_conv_bo)
    x = x + _L1_conv_ref(_gn(x), L1_conv_filt)
    return x

_drawn_inputs = setup_inputs


def setup_inputs(seed=0):
    import zlib

    import numpy as np

    out = dict(_drawn_inputs(seed))
    spreads = {}
    factors = {}
    for name, (base, spread) in spreads.items():
        noise = np.random.default_rng([zlib.crc32(name.encode()), seed]).standard_normal(out[name].shape)
        drawn = base * np.exp(spread * noise) if base else spread * noise
        out[name] = jnp.asarray(drawn.astype(out[name].dtype))
    for name, factor in factors.items():
        out[name] = (out[name] * factor).astype(out[name].dtype)
    return out
```

```python
import numpy as np

import concourse.bass as bass
from concourse import mybir
from contextlib import ExitStack


def shape_constants():
    p = np.arange(128)
    pair = (p % 32) // 2
    ident = np.eye(128, dtype=np.float32)
    average = (pair[:, None] == pair[None, :]).astype(np.float32) / 8
    eighths = np.full((128, 128), 0.125, np.float32)
    select = (pair[:, None] == np.arange(16)[None, :]).astype(np.float32)
    return np.concatenate([ident, average, eighths, select], axis=1)


def preact_pair_mix_blur(nc, x, filt, weights, bias_cols, bias_rows, consts, out):
    fp32 = mybir.dt.float32
    ALU = mybir.AluOpType
    ACT = mybir.ActivationFunctionType

    B, C, H, D = x.shape
    PAIRS = B * C // 2
    WAVES = 4
    WP = PAIRS // WAVES
    GP = 8
    CH = GP // 2
    GROUPS = PAIRS // GP
    Q = 128 // (2 * WP)
    ROWS = H // Q
    SLABS = 2 * WP
    EPS = 1e-5

    x_nat = x.rearrange("b (g t) j d -> (t j) (b g) d", t=2)
    mid = nc.dram_tensor("x1_scratch", (B, C, H, D), fp32, kind="Internal").ap()
    mid_nat = mid.rearrange("b (g t) j d -> (t j) (b g) d", t=2)

    def wave_of(t, w):
        b, h = divmod(w, WAVES // B)
        return t[b, h * SLABS:(h + 1) * SLABS, :, :]

    def slab_view(t, w):
        return wave_of(t, w).rearrange("s (q r) d -> q s (r d)", q=Q)

    ctx = ExitStack()
    with ctx:
        def sb(name, shape):
            return ctx.enter_context(nc.sbuf_tensor(name, shape, fp32))

        def pb(name, shape):
            return ctx.enter_context(nc.psum_tensor(name, shape, fp32))

        def sem(name):
            return ctx.enter_context(nc.semaphore(name))

        const = sb("const", [128, 400])
        ident, average = const[:, 0:128], const[:, 128:256]
        eighths, select = const[:, 256:384], const[:, 384:400]
        wbd = sb("wbd", [128, 4, 128])
        W_A, W_G, W_B, W_O = (wbd[:, n, :] for n in range(4))
        bcol = sb("bcol", [128, 2])
        brow = sb("brow", [128, 2, D])
        ftap = sb("ftap", [128, 2, 16])
        fsum = sb("fsum", [128, 2, 2])
        xslab = sb("xslab", [128, WAVES, ROWS * D])
        xnat = sb("xnat", [128, PAIRS, D])
        xn = sb("xn", [128, PAIRS, D])
        xb = sb("xb", [128, PAIRS, D])
        rt = sb("rt", [128, GROUPS, CH * 128])
        abd = sb("abd", [128, 2, CH, 2, 2, 64])
        bsb = sb("bsb", [128, GROUPS, CH, 128])
        gate = sb("gate", [128, GROUPS, CH * 128])
        zt = sb("zt", [128, GROUPS, CH * 128])
        x1 = sb("x1", [128, PAIRS, D])
        x1s = sb("x1s", [128, 2, ROWS + 1, D])
        y = sb("y", [128, 2, ROWS, D])
        stats = sb("stats", [128, 2, WAVES, 2, 6])
        mv = sb("mv", [128, 2, WAVES, 2])
        mean = sb("mean", [128, 2, WAVES])
        dev = sb("dev", [128, 2, WAVES])
        spread = sb("spread", [128, 2, WAVES])
        veps = sb("veps", [128, 2, WAVES])
        rstd = sb("rstd", [128, 2, WAVES])
        nmr = sb("nmr", [128, 2, WAVES])
        sel = sb("sel", [128, WAVES, 2, WP])
        scal = sb("scal", [128, WAVES, 2, WP])
        coef = sb("coef", [128, 2, 6])
        half = sb("half", [128, WAVES])

        ps_t = pb("ps_t", [128, 512])
        ps_a = pb("ps_a", [128, 512])
        ps_b = pb("ps_b", [128, 512])
        ps_g = pb("ps_g", [128, 512])
        ps_ab = pb("ps_ab", [128, 512])
        ps_o = pb("ps_o", [128, 512])
        ps_s = pb("ps_s", [128, 512])

        const_in, weights_in, filt_in = sem("const_in"), sem("weights_in"), sem("filt_in")
        slab_in = [sem(f"slab_in{w}") for w in range(WAVES)]
        nat_in = [sem(f"nat_in{w}") for w in range(WAVES)]
        mid_out = [sem(f"mid_out{w}") for w in range(WAVES)]
        mid_in = [sem(f"mid_in{w}") for w in range(WAVES)]
        stored = [sem(f"stored{w}") for w in range(WAVES)]
        zeros_set = sem("zeros_set")
        abd_zeroed = sem("abd_zeroed")
        dve_step = sem("dve_step")
        to_stat = sem("to_stat")
        stat_done = sem("stat_done")
        veps_done, rstd_done = sem("veps_done"), sem("rstd_done")
        scal_ready = sem("scal_ready")
        norm_pool, norm_dve, norm_act = sem("norm_pool"), sem("norm_dve"), sem("norm_act")
        xb_ready = sem("xb_ready")
        t_done, rt_ready = sem("t_done"), sem("rt_ready")
        a_done, abd_ready = sem("a_done"), sem("abd_ready")
        b_done, bsb_ready = sem("b_done"), sem("bsb_ready")
        g_done, gate_ready = sem("g_done"), sem("gate_ready")
        ab_done, zt_ready = sem("ab_done"), sem("zt_ready")
        o_done, x1_ready = sem("o_done"), sem("x1_ready")
        coef_ready, base_ready, y_ready = sem("coef_ready"), sem("base_ready"), sem("y_ready")

        block = ctx.enter_context(nc.Block())

        XJOBS = [range(0, 1), range(1, WAVES)]
        job_first = [0, 3] + [6 + 2 * w for w in range(WAVES)]
        POOL0, DVE0, ACT0 = range(0, 3), range(3, 6), range(6, 8)

        @block.sync
        def _(sp):
            for w in range(WAVES):
                sp.dma_start(xslab[:, w, :], slab_view(x, w)).then_inc(slab_in[w], 16)
                sp.dma_start(xnat[:, w * WP:(w + 1) * WP, :],
                             x_nat[:, w * WP:(w + 1) * WP, :]).then_inc(nat_in[w], 16)

            def store(w):
                sp.wait_ge(y_ready, w + 1)
                sp.dma_start(slab_view(out, w),
                             y[:, w % 2, :, :].rearrange("p r d -> p (r d)")).then_inc(stored[w], 16)

            for w in range(WAVES):
                for n in range(2):
                    g = 2 * w + n
                    sp.wait_ge(x1_ready, g + 1)
                    sp.dma_start(mid_nat[:, g * GP:(g + 1) * GP, :],
                                 x1[:, g * GP:(g + 1) * GP, :]).then_inc(mid_out[w], 16)
                    if n == 0 and w >= 2:
                        store(w - 2)
                sp.wait_ge(mid_out[w], 32)
                if w >= 2:
                    sp.wait_ge(y_ready, w - 1)
                rows = wave_of(mid, w)
                for q in range(Q):
                    n = ROWS + 1 if q < Q - 1 else ROWS
                    sp.dma_start(x1s[q * SLABS:(q + 1) * SLABS, w % 2, 0:n, :],
                                 rows[:, q * ROWS:q * ROWS + n, :]).then_inc(mid_in[w], 16)
            for w in range(WAVES - 2, WAVES):
                store(w)
            for w in range(WAVES):
                sp.wait_ge(stored[w], 16)

        @block.gpsimd
        def _(pool):
            nc.gpsimd.memset(wbd[0:64, :, 64:128], 0.0).then_inc(zeros_set, 1)
            pool.wait_ge(zeros_set, 1)
            nc.gpsimd.memset(wbd[64:128, :, 0:64], 0.0).then_inc(zeros_set, 1)
            pool.wait_ge(zeros_set, 2)
            nc.gpsimd.memset(half[:], -0.5).then_inc(zeros_set, 1)
            pool.wait_ge(zeros_set, 3)

            def inverse_root(job, k, ws):
                pool.wait_ge(veps_done, job + 1)
                nc.gpsimd.tensor_tensor(rstd[:, k, ws.start:ws.stop], veps[:, k, ws.start:ws.stop],
                                        half[:, 0:len(ws)], ALU.pow).then_inc(rstd_done, 1)

            def normalise(pairs):
                for p in pairs:
                    w, n = divmod(p, WP)
                    last = nc.gpsimd.tensor_scalar(xn[:, p, :], xnat[:, p, :], scal[:, w, 0, n:n + 1],
                                                   scal[:, w, 1, n:n + 1], ALU.mult, ALU.add)
                last.then_inc(norm_pool, 1)

            def add_bo(g):
                nc.gpsimd.tensor_tensor(
                    xb[:, g * GP:(g + 1) * GP, :], xnat[:, g * GP:(g + 1) * GP, :],
                    brow[:, 1:2, :].broadcast_to([128, GP, D]), ALU.add).then_inc(xb_ready, 1)

            inverse_root(0, 0, XJOBS[0])
            pool.wait_ge(nat_in[0], 16)
            pool.wait_ge(scal_ready, 1)
            normalise(POOL0)
            normalise(range(GP, 2 * GP))
            pool.wait_ge(weights_in, 16 * 6)
            inverse_root(1, 0, XJOBS[1])
            add_bo(0)
            pool.wait_ge(scal_ready, 2)
            for g in range(2, GROUPS):
                if g % 2 == 0:
                    pool.wait_ge(nat_in[g // 2], 16)
                normalise(range(g * GP, (g + 1) * GP))
                add_bo(g - 1)
                if g % 2 == 1 and g >= 5:
                    inverse_root(2 + (g - 5) // 2, 1, range((g - 5) // 2, (g - 5) // 2 + 1))
            add_bo(GROUPS - 1)
            for w in range(2, WAVES):
                inverse_root(2 + w, 1, range(w, w + 1))

        @block.scalar
        def _(act):
            act.dma_start(const[:], consts).then_inc(const_in, 16)
            for h in range(2):
                half_ = slice(64 * h, 64 * h + 64)
                act.dma_start(wbd[half_, :, half_], weights).then_inc(weights_in, 16)
                act.dma_start(bcol[half_, :], bias_cols).then_inc(weights_in, 16)
            for n in range(2):
                act.dma_start(brow[:, n, :], bias_rows[n:n + 1, :].broadcast_to([128, D])).then_inc(weights_in, 16)
            for h in range(2):
                for q in range(Q):
                    act.dma_start(ftap[q * SLABS:(q + 1) * SLABS, h, :],
                                  filt[h * SLABS:(h + 1) * SLABS, :]).then_inc(filt_in, 16)

            act.wait_ge(scal_ready, 1)
            act.wait_ge(nat_in[0], 16)
            for p in ACT0:
                last = nc.scalar.activation(xn[:, p, :], xnat[:, p, :], ACT.Identity,
                                            bias=scal[:, 0, 1, p:p + 1], scale=scal[:, 0, 0, p:p + 1])
            last.then_inc(norm_act, 1)

            def transposed_out(g):
                act.wait_ge(t_done, g + 1)
                nc.scalar.activation(rt[:, g, :], ps_t[:], ACT.Copy).then_inc(rt_ready, 1)

            def a_out(g):
                act.wait_ge(a_done, g + 1)
                if g >= 2:
                    act.wait_ge(ab_done, g - 1)
                src = ps_a[:].rearrange("p (c t j) -> p c t j", c=CH, t=2)
                for p2 in range(2):
                    for i2 in range(2):
                        last = nc.scalar.activation(
                            abd[64 * i2:64 * i2 + 64, g % 2, :, p2, i2, :],
                            src[64 * p2:64 * p2 + 64, :, i2, :], ACT.Identity,
                            bias=bcol[64 * p2:64 * p2 + 64, 0:1])
                last.then_inc(abd_ready, 1)

            def gate_out(g):
                act.wait_ge(g_done, g + 1)
                nc.scalar.activation(gate[:, g, :], ps_g[:], ACT.Sigmoid,
                                     bias=bcol[:, 1:2]).then_inc(gate_ready, 1)

            def filter_base(w):
                act.wait_ge(coef_ready, w + 1)
                if w >= 2:
                    act.wait_ge(stored[w - 2], 16)
                nc.scalar.activation(y[:, w % 2, :, :], x1s[:, w % 2, 0:ROWS, :], ACT.Identity,
                                     bias=coef[:, w % 2, 4:5], scale=coef[:, w % 2, 0:1]).then_inc(base_ready, 1)

            act.wait_ge(weights_in, 16 * 6)
            act.wait_ge(abd_zeroed, 1)
            transposed_out(0)
            for g in range(GROUPS):
                a_out(g)
                gate_out(g)
                if g + 1 < GROUPS:
                    transposed_out(g + 1)
                if g >= 4 and g % 2 == 0:
                    filter_base((g - 4) // 2)
            for w in range(WAVES - 2, WAVES):
                filter_base(w)

        @block.vector
        def _(dve):
            steps = [0]

            def link(ins):
                steps[0] += 1
                ins.then_inc(dve_step, 1)
                dve.wait_ge(dve_step, steps[0])

            products = [0]

            def product_done():
                products[0] += 1
                dve.wait_ge(stat_done, products[0])

            def partition_stats(k, w, src):
                for n in range(2):
                    last = nc.vector.bn_stats(stats[:, k, w, n, :], src[:, n * 512:(n + 1) * 512])
                link(last)
                return nc.vector.bn_aggr(mv[:, k, w, :], stats[:, k, w, :, :].rearrange("p a b -> p (a b)"))

            def group_stats(k, ws):
                s = slice(ws.start, ws.stop)
                n = len(ws)
                product_done()
                link(nc.vector.tensor_copy(mean[:, k, s], ps_s[:, 0:n]))
                link(nc.vector.tensor_tensor(dev[:, k, s], mv[:, k, s, 0], mean[:, k, s], ALU.subtract))
                link(nc.vector.tensor_tensor(dev[:, k, s], dev[:, k, s], dev[:, k, s], ALU.mult))
                nc.vector.tensor_tensor(spread[:, k, s], dev[:, k, s], mv[:, k, s, 1], ALU.add).then_inc(to_stat, 1)
                product_done()
                nc.vector.tensor_scalar_add(veps[:, k, s], ps_s[:, 0:n], EPS).then_inc(veps_done, 1)

            def minus_mean_rstd(job, k, ws):
                s = slice(ws.start, ws.stop)
                dve.wait_ge(rstd_done, job + 1)
                link(nc.vector.scalar_tensor_tensor(nmr[:, k, s], mean[:, k, s], -1.0, rstd[:, k, s],
                                                    ALU.mult, ALU.mult))

            def select_pairs(ws):
                for w in ws:
                    nc.vector.tensor_scalar(sel[:, w, 0, :], select, rstd[:, 0, w:w + 1], None, ALU.mult)
                    last = nc.vector.tensor_scalar(sel[:, w, 1, :], select, nmr[:, 0, w:w + 1], None, ALU.mult)
                last.then_inc(to_stat, 1)

            def scalars_out(ws):
                product_done()
                n = len(ws) * 2 * WP
                nc.vector.tensor_copy(scal[:, ws.start:ws.stop, :, :].rearrange("p w k n -> p (w k n)"),
                                      ps_s[:, 0:n]).then_inc(scal_ready, 1)

            def b_out(g):
                dve.wait_ge(b_done, g + 1)
                nc.vector.tensor_tensor(
                    bsb[:, g, :, :].rearrange("p c (t l) -> p (c t) l", t=2),
                    ps_b[:].rearrange("p (n l) -> p n l", l=D),
                    brow[:, 0:1, :].broadcast_to([128, GP, D]), ALU.add).then_inc(bsb_ready, 1)

            def z_out(g):
                dve.wait_ge(gate_ready, g + 1)
                dve.wait_ge(ab_done, g + 1)
                nc.vector.tensor_tensor(zt[:, g, :], ps_ab[:], gate[:, g, :], ALU.mult).then_inc(zt_ready, 1)

            def x1_out(g):
                dve.wait_ge(o_done, g + 1)
                dve.wait_ge(xb_ready, g + 1)
                nc.vector.tensor_tensor(
                    x1[:, g * GP:(g + 1) * GP, :], ps_o[:].rearrange("p (n e) -> p n e", e=D),
                    xb[:, g * GP:(g + 1) * GP, :], ALU.add).then_inc(x1_ready, 1)

            def filter_stats(w):
                dve.wait_ge(mid_in[w], 16 * Q)
                partition_stats(1, w, x1s[:, w % 2, 0:ROWS, :].rearrange("p r d -> p (r d)")).then_inc(to_stat, 1)

            def filter_coefs(w):
                h, r = w % 2, w % 2
                minus_mean_rstd(2 + w, 1, range(w, w + 1))
                nc.vector.tensor_copy(x1s[(Q - 1) * SLABS:128, r, ROWS, :],
                                      mean[(Q - 1) * SLABS:128, 1, w:w + 1].broadcast_to([SLABS, D]))
                nc.vector.tensor_scalar(coef[:, r, 4:6], fsum[:, h, :], nmr[:, 1, w:w + 1], None, ALU.mult)
                taps = ftap[:, h, :].rearrange("p (a b) -> p a b", a=4)[:, 1:4:2, 1:4:2]
                link(nc.vector.tensor_scalar(coef[:, r, 0:4].rearrange("p (a b) -> p a b", a=2), taps,
                                             rstd[:, 1, w:w + 1], None, ALU.mult))
                nc.vector.tensor_scalar_add(coef[:, r, 0:1], coef[:, r, 0:1], 1.0).then_inc(coef_ready, 1)

            def filter_taps(w):
                r = w % 2
                dve.wait_ge(base_ready, w + 1)
                whole, left, edge = y[:, r, :, :], y[:, r, :, 0:D - 1], y[:, r, :, D - 1:D]
                here, below = x1s[:, r, 0:ROWS, :], x1s[:, r, 1:ROWS + 1, :]
                link(nc.vector.scalar_tensor_tensor(left, here[:, :, 1:D], coef[:, r, 1:2], left, ALU.mult, ALU.add))
                link(nc.vector.tensor_scalar(edge, edge, coef[:, r, 5:6], None, ALU.add))
                link(nc.vector.scalar_tensor_tensor(whole, below, coef[:, r, 2:3], whole, ALU.mult, ALU.add))
                nc.vector.scalar_tensor_tensor(left, below[:, :, 1:D], coef[:, r, 3:4], left, ALU.mult,
                                               ALU.add).then_inc(y_ready, 1)

            for r in range(2):
                nc.vector.memset(abd[0:64, r, :, :, 1, :], 0.0)
                last = nc.vector.memset(abd[64:128, r, :, :, 0, :], 0.0)
            last.then_inc(abd_zeroed, 1)
            for job, ws in enumerate(XJOBS[:1]):
                dve.wait_ge(slab_in[0], 16)
                partition_stats(0, 0, xslab[:, 0, :]).then_inc(to_stat, 1)
                group_stats(0, ws)
                minus_mean_rstd(0, 0, ws)
                dve.wait_ge(const_in, 16)
                select_pairs(ws)
                scalars_out(ws)
            dve.wait_ge(dve_step, steps[0])
            dve.wait_ge(scal_ready, 1)
            dve.wait_ge(nat_in[0], 16)
            for p in DVE0:
                last = nc.vector.tensor_scalar(xn[:, p, :], xnat[:, p, :], scal[:, 0, 0, p:p + 1],
                                               scal[:, 0, 1, p:p + 1], ALU.mult, ALU.add)
            last.then_inc(norm_dve, 1)
            for w in XJOBS[1]:
                dve.wait_ge(slab_in[w], 16)
                last = partition_stats(0, w, xslab[:, w, :])
            last.then_inc(to_stat, 1)
            dve.wait_ge(filt_in, 16 * 2 * Q)
            for h in range(2):
                taps = ftap[:, h, :].rearrange("p (a b) -> p a b", a=4)[:, 1:4:2, 1:4:2]
                nc.vector.tensor_reduce(fsum[:, h, 0:1], taps, mybir.AxisListType.XY, ALU.add)
                link(nc.vector.tensor_reduce(fsum[:, h, 1:2], taps[:, :, 1:2], mybir.AxisListType.XY, ALU.add))
                link(nc.vector.tensor_scalar(fsum[:, h, 1:2], fsum[:, h, 1:2], -1.0, None, ALU.mult))
            dve.wait_ge(weights_in, 16 * 6)
            for g in range(GROUPS + 1):
                if g < GROUPS:
                    b_out(g)
                if g == 0:
                    group_stats(0, XJOBS[1])
                    minus_mean_rstd(1, 0, XJOBS[1])
                    select_pairs(XJOBS[1])
                    scalars_out(XJOBS[1])
                if g >= 1:
                    x1_out(g - 1)
                if g < GROUPS:
                    z_out(g)
                if g >= 3 and g % 2 == 1:
                    filter_stats((g - 3) // 2)
                    group_stats(1, range((g - 3) // 2, (g - 3) // 2 + 1))
                    filter_coefs((g - 3) // 2)
                if g >= 4 and g % 2 == 0:
                    filter_taps((g - 4) // 2)
            for w in range(WAVES - 1, WAVES):
                filter_stats(w)
                group_stats(1, range(w, w + 1))
                filter_coefs(w)
                filter_taps(w)

        @block.tensor
        def _(pe):
            stat = [0]

            def stat_product(lhs, rhs, n):
                stat[0] += 1
                pe.wait_ge(to_stat, stat[0])
                nc.tensor.matmul(ps_s[:, 0:n], lhs, rhs, start=True, stop=True).then_inc(stat_done, 1)

            def transposes(g):
                if g == 0:
                    pe.wait_ge(norm_dve, 1)
                    pe.wait_ge(norm_act, 1)
                pe.wait_ge(norm_pool, g + 1)
                if g >= 1:
                    pe.wait_ge(rt_ready, g)
                for c in range(CH):
                    p = g * GP + 2 * c
                    last = nc.tensor.transpose(ps_t[:, c * 128:(c + 1) * 128],
                                               xn[:, p:p + 2, :].rearrange("p n d -> p (n d)"), ident)
                last.then_inc(t_done, 1)

            def product_a(g):
                pe.wait_ge(rt_ready, g + 1)
                if g >= 1:
                    pe.wait_ge(abd_ready, g)
                nc.tensor.matmul(ps_a[:], W_A, rt[:, g, :], start=True, stop=True).then_inc(a_done, 1)

            def product_b(g):
                if g >= 1:
                    pe.wait_ge(bsb_ready, g)
                for c in range(CH):
                    last = nc.tensor.matmul(ps_b[:, c * 128:(c + 1) * 128], rt[:, g, c * 128:(c + 1) * 128], W_B,
                                            start=True, stop=True)
                last.then_inc(b_done, 1)

            def product_g(g):
                if g >= 1:
                    pe.wait_ge(gate_ready, g)
                nc.tensor.matmul(ps_g[:], W_G, rt[:, g, :], start=True, stop=True).then_inc(g_done, 1)

            def product_ab(g):
                pe.wait_ge(abd_ready, g + 1)
                pe.wait_ge(bsb_ready, g + 1)
                if g >= 1:
                    pe.wait_ge(zt_ready, g)
                for c in range(CH):
                    for p2 in range(2):
                        last = nc.tensor.matmul(
                            ps_ab[64 * p2:64 * p2 + 64, c * 128:(c + 1) * 128],
                            bsb[:, g, c, 64 * p2:64 * p2 + 64],
                            abd[:, g % 2, c, p2, :, :].rearrange("p t j -> p (t j)"), start=True, stop=True)
                last.then_inc(ab_done, 1)

            def product_o(g):
                pe.wait_ge(zt_ready, g + 1)
                if g >= 1:
                    pe.wait_ge(x1_ready, g)
                for c in range(CH):
                    last = nc.tensor.matmul(ps_o[:, c * 128:(c + 1) * 128], zt[:, g, c * 128:(c + 1) * 128], W_O,
                                            start=True, stop=True)
                last.then_inc(o_done, 1)

            def stats_of(k, ws, part):
                s = slice(ws.start, ws.stop)
                if part == 0:
                    stat_product(average, mv[:, k, s, 0], len(ws))
                elif part == 1:
                    stat_product(average, spread[:, k, s], len(ws))
                else:
                    stat_product(eighths, sel[:, s, :, :].rearrange("p w k n -> p (w k n)"), len(ws) * 2 * WP)

            pe.wait_ge(const_in, 16)
            for part in range(3):
                stats_of(0, XJOBS[0], part)
            transposes(0)
            stats_of(0, XJOBS[1], 0)
            pe.wait_ge(weights_in, 16 * 6)
            pe.wait_ge(zeros_set, 2)
            for g in range(GROUPS + 1):
                w = (g - 3) // 2
                if g < GROUPS:
                    product_a(g)
                    product_b(g)
                    product_g(g)
                if g == 0:
                    stats_of(0, XJOBS[1], 1)
                if g + 1 < GROUPS and g == 0:
                    transposes(g + 1)
                    stats_of(0, XJOBS[1], 2)
                elif g + 1 < GROUPS:
                    transposes(g + 1)
                if g >= 1:
                    product_o(g - 1)
                if g < GROUPS:
                    product_ab(g)
                if g >= 3 and g % 2 == 1:
                    stats_of(1, range(w, w + 1), 0)
                    stats_of(1, range(w, w + 1), 1)
            w = WAVES - 1
            stats_of(1, range(w, w + 1), 0)
            stats_of(1, range(w, w + 1), 1)


_BLUR_TAPS = 16


def kernel(x, L0_conv_Wa, L0_conv_ba, L0_conv_Wb, L0_conv_bb, L0_conv_Wg, L0_conv_bg, L0_conv_Wo, L0_conv_bo,
           L1_conv_filt):
    import concourse.bacc as _bacc
    from concourse.bass_utils import run_bass_kernel_spmd as _run

    c = np.ascontiguousarray
    arrays = {
        "x": c(x),
        "filt": c(np.asarray(L1_conv_filt).reshape(-1, _BLUR_TAPS)),
        "weights": c(np.stack([L0_conv_Wa, L0_conv_Wg, L0_conv_Wb, L0_conv_Wo], axis=1)),
        "bias_cols": c(np.stack([L0_conv_ba, L0_conv_bg], axis=1)),
        "bias_rows": c(np.stack([L0_conv_bb, L0_conv_bo], axis=0)),
        "consts": shape_constants(),
    }
    nc = _bacc.Bacc("TRN2", target_bir_lowering=False, num_devices=1)
    args = [nc.dram_tensor(n, a.shape, mybir.dt.from_np(a.dtype), kind="ExternalInput").ap()
            for n, a in arrays.items()]
    out = nc.dram_tensor("out", arrays["x"].shape, mybir.dt.float32, kind="ExternalOutput").ap()
    preact_pair_mix_blur(nc, *args, out)
    return _run(nc, [arrays], core_ids=[0]).results[0]["out"]
```

```python
import numpy as np

import concourse.bass as bass
from concourse import mybir
from contextlib import ExitStack

BLOCKS = 8
ROWS = 8
CHUNKS = 8
TAPS = 16


def mask_columns():
    p = np.arange(128)
    chunk = p // 16
    average = (chunk[:, None] == chunk[None, :]) / 16.0
    spread = np.full((128, 64), 1 / 16.0)
    select = chunk[:, None] == np.arange(CHUNKS)[None, :]
    last = p % BLOCKS == BLOCKS - 1
    above = (p[:, None] == p[None, :] + 1) & ~last[None, :]
    return [m.astype(np.float32) for m in (average, spread, select, np.eye(128), above, last[:, None])]


def parameter_columns(Wa, ba, Wb, bb, Wg, bg, Wo, bo, filt):
    weights = np.zeros((128, 4, 128), np.float32)
    for n, m in enumerate((Wa, Wg, Wb, Wo)):
        weights[:64, n, :64] = m
        weights[64:, n, 64:] = m
    cols = np.tile(np.stack([ba, bg], axis=1), (2, 1))
    rows = np.tile(np.concatenate([bb, bo])[None, :], (128, 1))
    taps = filt.reshape(2, CHUNKS, 2, 2, TAPS).transpose(1, 3, 0, 2, 4).reshape(16, 4 * TAPS)
    return [weights.reshape(128, 512), cols, rows, np.repeat(taps, BLOCKS, axis=0)]


def preact_pair_mix_blur(nc, x, params, out):
    fp32 = mybir.dt.float32
    ALU = mybir.AluOpType
    ACT = mybir.ActivationFunctionType

    B, C, H, D = x.shape
    WP = 2 * CHUNKS
    PAIRS = B * C // 2
    WAVES = PAIRS // WP
    CH = CHUNKS // 2
    GP = 2 * CH
    GROUPS = PAIRS // GP
    EPS = 1e-5

    x_nat = x.rearrange("b (g t) j d -> (t j) (b g) d", t=2)

    def slab_view(t, w, p2):
        b, h = divmod(w, WAVES // B)
        return t[b, h * 2 * WP:(h + 1) * 2 * WP, :, :].rearrange(
            "(c p t) (q r) d -> p c (t q) (r d)", p=2, t=2, q=BLOCKS)[p2]

    ctx = ExitStack()
    with ctx:
        def sb(name, shape):
            return ctx.enter_context(nc.sbuf_tensor(name, shape, fp32))

        def pb(name, shape):
            return ctx.enter_context(nc.psum_tensor(name, shape, fp32))

        def sem(name):
            return ctx.enter_context(nc.semaphore(name))

        par = sb("par", [128, params.shape[1]])
        ends = np.cumsum([0, 128, 64, CHUNKS, 128, 128, 1, 4 * 128, 2, 2 * D, 4 * TAPS]).tolist()
        average, spread, select, ident, above, last_block, wbd, bcol, brow, ftap = (
            par[:, a:b] for a, b in zip(ends, ends[1:]))
        MASKS = ends[6]
        W_A, W_G, W_B, W_O = (wbd[:, 128 * n:128 * n + 128] for n in range(4))
        bb = brow[:, 0:D].rearrange("p (n d) -> p n d", n=1)
        bo = brow[:, D:2 * D].rearrange("p (n d) -> p n d", n=1)
        ftap = ftap.rearrange("p (n a b) -> p n a b", a=4, b=4)
        own_taps = sb("own_taps", [128, 2, 2, 6])
        xs = sb("xs", [128, WAVES, 2, ROWS, D])
        xnat = sb("xnat", [128, PAIRS, D])
        xb = sb("xb", [128, WAVES, 2, ROWS, D])
        rt = sb("rt", [128, GROUPS, CH * 128])
        abd = sb("abd", [128, 2, CH, 2, 2, 64])
        bsb = sb("bsb", [128, 2, CH, 128])
        gate = sb("gate", [128, 2, CH * 128])
        zt = sb("zt", [128, WAVES, ROWS, 128])
        x1 = sb("x1", [128, WAVES, 2, ROWS + 1, D])
        y = sb("y", [128, WAVES, 2, ROWS, D])
        prod = sb("prod", [128, WAVES - 1, 2, 3, ROWS, D])
        part = sb("part", [128, 2, WAVES, 2, 2, 6])
        mv = sb("mv", [128, 2, WAVES, 2, 2])
        mean = sb("mean", [128, 2, WAVES, 2])
        dev = sb("dev", [128, 2, WAVES, 2])
        second = sb("second", [128, 2, WAVES, 2])
        veps = sb("veps", [128, 2, WAVES, 2])
        norm = sb("norm", [128, 2, WAVES, 2, 2])
        sel = sb("sel", [128, 2, WAVES, 2, CHUNKS])
        share = sb("share", [128, 2, WAVES, 2, CHUNKS])
        scal = sb("scal", [128, WAVES, 2, CHUNKS])
        coef = sb("coef", [128, WAVES, 2, 6])
        pad = sb("pad", [128, WAVES, 2])
        offs = sb("offs", [128, 2, 2])
        diag = sb("diag", [128, TAPS // 4, 128])
        half = sb("half", [128, 2 * WAVES])
        warm = sb("warm", [128, 1])
        zeros = sb("zeros", [128, 128])

        ps_t = pb("ps_t", [128, 512])
        ps_a = pb("ps_a", [128, 512])
        ps_b = pb("ps_b", [128, 512])
        ps_g = pb("ps_g", [128, 512])
        ps_ab = pb("ps_ab", [128, 512])
        ps_o = pb("ps_o", [128, 1024])
        ps_s = pb("ps_s", [128, 512])
        ps_stat = ps_s[:, 0:128]
        ps_row = ps_o[:, 0:128]

        masks_in, params_in = sem("masks_in"), sem("params_in")
        xs_in = [[sem(f"xs_in{w}_{p2}") for p2 in range(2)] for w in range(WAVES)]
        nat_in = [sem(f"nat_in{g}") for g in range(GROUPS)]
        stored = sem("stored")
        half_set, abd_zeroed = sem("half_set"), sem("abd_zeroed")
        zeros_set = sem("zeros_set")
        dve_step = sem("dve_step")
        to_stat, stat_done = sem("to_stat"), sem("stat_done")
        stat_read = sem("stat_read")
        rstd_done = sem("rstd_done")
        taps_ready, diag_ready = sem("taps_ready"), sem("diag_ready")
        xb_ready = sem("xb_ready")
        t_done, rt_ready, rt0_dve = sem("t_done"), sem("rt_ready"), sem("rt0_dve")
        a_done, abd_ready = sem("a_done"), sem("abd_ready")
        b_done, bsb_ready = sem("b_done"), sem("bsb_ready")
        g_done, gate_ready = sem("g_done"), sem("gate_ready")
        ab_done, zt_ready = sem("ab_done"), sem("zt_ready")
        o_done, x1_ready = sem("o_done"), sem("x1_ready")
        row_done, row_ready = sem("row_done"), sem("row_ready")
        coef_ready, base_ready = sem("coef_ready"), sem("base_ready")
        pool_tap = sem("pool_tap")
        y_pool, y_dve = sem("y_pool"), sem("y_dve")
        prod_ready = sem("prod_ready")
        offs_ready, last_base = sem("offs_ready"), sem("last_base")
        sum_pe, last_sum_ready = sem("sum_pe"), sem("last_sum_ready")

        block = ctx.enter_context(nc.Block())

        XJOBS = [range(0, 1), range(1, 2), range(2, WAVES)]
        X1JOB = len(XJOBS)
        STATS = [(0, 0), (0, 1), (0, 2), (1, 0), (1, 1), (1, 2), (2, 0), (2, 1), (2, 2)]
        STATS += [(X1JOB + w, step) for w in range(WAVES) for step in range(2)]

        def nth(job, step):
            return STATS.index((job, step)) + 1

        WARM = (8, 2, 2, 3)
        DVE0 = range(2, 4)

        def scalar_of(g, c, k):
            n = CH * (g % 2) + c
            return scal[:, g // 2, k, n:n + 1]

        @block.sync
        def _(sp):
            def load_slab(w):
                for p2 in range(2):
                    sp.dma_start(xs[:, w, p2, :, :].rearrange("p r d -> p (r d)"),
                                 slab_view(x, w, p2)).then_inc(xs_in[w][p2], 16)

            def load_nat(g):
                sp.dma_start(xnat[:, g * GP:(g + 1) * GP, :],
                             x_nat[:, g * GP:(g + 1) * GP, :]).then_inc(nat_in[g], 16)

            load_slab(0)
            sp.dma_start(par[:, 0:MASKS], params[:, 0:MASKS]).then_inc(masks_in, 16)
            load_nat(0)
            sp.dma_start(par[:, MASKS:], params[:, MASKS:]).then_inc(params_in, 16)
            load_slab(1)
            load_nat(1)
            load_nat(2)
            load_slab(2)
            load_slab(3)
            for g in range(3, GROUPS):
                load_nat(g)
            for w in range(WAVES):
                for p2 in range(2):
                    if w == WAVES - 2:
                        sp.wait_ge(y_pool, 2 * w + p2 + 1)
                    else:
                        sp.wait_ge(y_dve, 2 * w + p2 + 1 if w < WAVES - 2 else 2 * (w - 1) + p2 + 1)
                    sp.dma_start(slab_view(out, w, p2),
                                 y[:, w, p2, :, :].rearrange("p r d -> p (r d)")).then_inc(stored, 16)
            sp.wait_ge(stored, 16 * 2 * WAVES)

        @block.gpsimd
        def _(pool):
            nc.gpsimd.memset(half[:], -0.5).then_inc(half_set, 1)
            pool.wait_ge(half_set, 1)

            def inverse_root(job, k, ws):
                pool.wait_ge(stat_read, nth(job, 1))
                v = veps[:, k, ws.start:ws.stop, :].rearrange("p w n -> p (w n)")
                nc.gpsimd.tensor_tensor(norm[:, k, ws.start:ws.stop, 0, :], v.rearrange("p (w n) -> p w n", n=2),
                                        half[:, 0:2 * len(ws)].rearrange("p (w n) -> p w n", n=2),
                                        ALU.pow).then_inc(rstd_done, 1)

            def x1_inverse_root(w):
                inverse_root(X1JOB + w, 1, range(w, w + 1))

            def add_bo(w):
                for p2 in range(2):
                    pool.wait_ge(xs_in[w][p2], 16)
                    nc.gpsimd.tensor_tensor(xb[:, w, p2, :, :], xs[:, w, p2, :, :],
                                            bo.broadcast_to([128, ROWS, D]), ALU.add).then_inc(xb_ready, 1)

            taps_done = [0]

            def link(ins):
                taps_done[0] += 1
                ins.then_inc(pool_tap, 1)
                pool.wait_ge(pool_tap, taps_done[0])

            def right_product(w):
                pool.wait_ge(coef_ready, w + 1)
                link(nc.gpsimd.tensor_scalar(prod[:, w, 0, 0, :, 0:D - 1], x1[:, w, 0, 0:ROWS, 1:D],
                                             coef[:, w, 0, 1:2], None, ALU.mult))

            def edge_and_right(w, p2, right):
                pool.wait_ge(base_ready, 2 * w + p2 + 1)
                left, edge = y[:, w, p2, :, 0:D - 1], y[:, w, p2, :, D - 1:D]
                nc.gpsimd.tensor_scalar(edge, edge, coef[:, w, p2, 5:6], None, ALU.add)
                if right:
                    link(nc.gpsimd.tensor_tensor(left, left, prod[:, w, p2, 0, :, 0:D - 1], ALU.add))

            def below_right(w, p2, n):
                pool.wait_ge(prod_ready, n)
                left = y[:, w, p2, :, 0:D - 1]
                nc.gpsimd.tensor_tensor(left, left, prod[:, w, p2, 2, :, 0:D - 1], ALU.add).then_inc(y_pool, 1)

            def all_taps(w, p2, steps):
                n = 2 * w + 3 * p2
                if 0 in steps:
                    pool.wait_ge(prod_ready, n + 1)
                    edge_and_right(w, p2, True)
                if 1 in steps:
                    pool.wait_ge(prod_ready, n + 2)
                    link(nc.gpsimd.tensor_tensor(y[:, w, p2, :, :], y[:, w, p2, :, :], prod[:, w, p2, 1, :, :],
                                                 ALU.add))
                    below_right(w, p2, n + 3)

            inverse_root(0, 0, XJOBS[0])
            pool.wait_ge(params_in, 16)
            add_bo(0)
            pool.wait_ge(taps_ready, 1)
            for n in range(TAPS // 4):
                last = nc.gpsimd.tensor_scalar(diag[:, n, :], ident, own_taps[:, (WAVES - 1) % 2, 1, n:n + 1], None,
                                               ALU.mult)
            last.then_inc(diag_ready, 1)
            inverse_root(1, 0, XJOBS[1])
            add_bo(1)
            add_bo(2)
            inverse_root(2, 0, XJOBS[2])
            add_bo(3)
            x1_inverse_root(0)
            for w in range(WAVES - 2):
                right_product(w)
                edge_and_right(w, 0, True)
                below_right(w, 0, 2 * w + 1)
                edge_and_right(w, 1, False)
                below_right(w, 1, 2 * w + 2)
                x1_inverse_root(w + 1)
            all_taps(WAVES - 2, 0, (0, 1))
            all_taps(WAVES - 2, 1, (0,))
            x1_inverse_root(WAVES - 1)
            all_taps(WAVES - 2, 1, (1,))

        @block.scalar
        def _(act):
            act.wait_ge(half_set, 1)
            nc.scalar.activation(warm[:], half[:, 0:1], ACT.Sigmoid)

            def transposed_out(g):
                act.wait_ge(t_done, g + 1)
                job = min(g // 2, 2)
                act.wait_ge(stat_read, nth(job, 2))
                chunks = range(CH) if g > 0 else range(DVE0.start)
                for c in chunks:
                    n = slice(c * 128, c * 128 + 128)
                    last = nc.scalar.activation(rt[:, g, n], ps_t[:, n], ACT.Identity,
                                                bias=scalar_of(g, c, 1), scale=scalar_of(g, c, 0))
                last.then_inc(rt_ready, 1)

            def a_out(g):
                act.wait_ge(a_done, g + 1)
                if g >= 2:
                    act.wait_ge(ab_done, g - 1)
                src = ps_a[:].rearrange("p (c t j) -> p c t j", c=CH, t=2)
                for p2 in range(2):
                    for i2 in range(2):
                        last = nc.scalar.activation(
                            abd[64 * i2:64 * i2 + 64, g % 2, :, p2, i2, :],
                            src[64 * p2:64 * p2 + 64, :, i2, :], ACT.Identity,
                            bias=bcol[64 * p2:64 * p2 + 64, 0:1])
                last.then_inc(abd_ready, 1)

            def gate_out(g):
                act.wait_ge(g_done, g + 1)
                if g >= 2:
                    act.wait_ge(zt_ready, g - 1)
                nc.scalar.activation(gate[:, g % 2, :], ps_g[:], ACT.Sigmoid,
                                     bias=bcol[:, 1:2]).then_inc(gate_ready, 1)

            def filter_base(w, p2):
                act.wait_ge(coef_ready, w + 1)
                nc.scalar.activation(y[:, w, p2, :, :], x1[:, w, p2, 0:ROWS, :], ACT.Identity,
                                     bias=coef[:, w, p2, 4:5], scale=coef[:, w, p2, 0:1]).then_inc(base_ready, 1)

            def filter_product(w, p2, k):
                row, col = (k + 1) // 2, (k + 1) % 2
                act.wait_ge(row_ready, w + 1)
                nc.scalar.activation(prod[:, w, p2, k, :, 0:D - col], x1[:, w, p2, row:row + ROWS, col:D], ACT.Copy,
                                     scale=coef[:, w, p2, k + 1:k + 2]).then_inc(prod_ready, 1)

            transposed_out(0)
            act.wait_ge(params_in, 16)
            act.wait_ge(abd_zeroed, 1)
            for g in range(GROUPS):
                a_out(g)
                if g + 1 < GROUPS:
                    transposed_out(g + 1)
                if g % 2 == 0 and g >= 4:
                    for p2 in range(2):
                        filter_base(g // 2 - 2, p2)
                gate_out(g)
                if g % 2 == 0 and g >= 4:
                    for p2 in range(2):
                        filter_product(g // 2 - 2, p2, 2)
            w = WAVES - 2
            filter_base(w, 0)
            filter_product(w, 0, 0)
            filter_base(w, 1)
            filter_product(w, 0, 1)
            filter_product(w, 0, 2)
            filter_product(w, 1, 0)
            filter_product(w, 1, 1)
            last = WAVES - 1
            act.wait_ge(offs_ready, 1)
            nc.scalar.activation(y[:, last, 0, :, :], x1[:, last, 0, 0:ROWS, :], ACT.Identity,
                                 bias=offs[:, 0, 0:1], scale=own_taps[:, last % 2, 0, 0:1]).then_inc(last_base, 1)
            filter_product(w, 1, 2)
            act.wait_ge(sum_pe, 1)
            nc.scalar.activation(y[:, last, 1, :, :], ps_a[:].rearrange("p (r d) -> p r d", d=D), ACT.Identity,
                                 bias=offs[:, 1, 0:1]).then_inc(last_sum_ready, 1)

        @block.vector
        def _(dve):
            steps = [0]

            def link(ins):
                steps[0] += 1
                ins.then_inc(dve_step, 1)
                dve.wait_ge(dve_step, steps[0])

            def product_done(job, step):
                dve.wait_ge(stat_done, nth(job, step))

            def partition_stats(k, ws, halves):
                for w in ws:
                    for p2 in range(2):
                        last = nc.vector.bn_aggr(
                            mv[:, k, w, p2, :], part[:, k, w, p2, 0:halves, :].rearrange("p a b -> p (a b)"))
                last.then_inc(to_stat, 1)

            def group_stats(job, k, ws):
                s = slice(ws.start, ws.stop)
                n = 2 * len(ws)
                ps = ps_stat[:, 0:n].rearrange("p (w n) -> p w n", n=2)
                product_done(job, 0)
                nc.vector.tensor_copy(mean[:, k, s, :], ps).then_inc(stat_read, 1)
                dve.wait_ge(stat_read, nth(job, 0))
                if job == X1JOB + WAVES - 1:
                    nc.vector.scalar_tensor_tensor(
                        offs[:], mean[:, 1, WAVES - 1, :].rearrange("p (n o) -> p n o", o=1).broadcast_to([128, 2, 2]),
                        -1.0, own_taps[:, (WAVES - 1) % 2, :, 4:6], ALU.mult, ALU.mult).then_inc(offs_ready, 1)
                link(nc.vector.tensor_tensor(dev[:, k, s, :], mv[:, k, s, :, 0], mean[:, k, s, :], ALU.subtract))
                link(nc.vector.tensor_tensor(dev[:, k, s, :], dev[:, k, s, :], dev[:, k, s, :], ALU.mult))
                nc.vector.tensor_tensor(second[:, k, s, :], dev[:, k, s, :], mv[:, k, s, :, 1],
                                        ALU.add).then_inc(to_stat, 1)

            def group_variance(job, k, ws):
                s = slice(ws.start, ws.stop)
                product_done(job, 1)
                nc.vector.tensor_scalar_add(veps[:, k, s, :],
                                            ps_stat[:, 0:2 * len(ws)].rearrange("p (w n) -> p w n", n=2),
                                            EPS).then_inc(stat_read, 1)

            def minus_mean_rstd(job, k, ws):
                s = slice(ws.start, ws.stop)
                dve.wait_ge(rstd_done, job + 1)
                link(nc.vector.scalar_tensor_tensor(norm[:, k, s, 1, :], mean[:, k, s, :], -1.0, norm[:, k, s, 0, :],
                                                    ALU.mult, ALU.mult))

            def x_stats(w):
                for p2 in range(2):
                    dve.wait_ge(xs_in[w][p2], 16)
                    last = nc.vector.bn_stats(part[:, 0, w, p2, 0, :], xs[:, w, p2, :, :].rearrange("p r d -> p (r d)"))
                link(last)

            def x_shares(job):
                for p2 in range(2):
                    for w in XJOBS[job]:
                        nc.vector.tensor_copy(share[:, p2, w, 0, :], select)
                        last = nc.vector.tensor_scalar(share[:, p2, w, 1, :], select, mean[:, 0, w, p2:p2 + 1], -1.0,
                                                       ALU.mult, ALU.mult)
                link(last)

            def x_scalars(job):
                ws = XJOBS[job]
                dve.wait_ge(rstd_done, job + 1)
                for w in ws:
                    last = nc.vector.tensor_tensor(
                        sel[:, :, w, :, :].rearrange("p n k c -> p n (k c)"),
                        share[:, :, w, :, :].rearrange("p n k c -> p n (k c)"),
                        norm[:, 0, w, 0, :].rearrange("p (n o) -> p n o", o=1).broadcast_to([128, 2, 2 * CHUNKS]),
                        ALU.mult)
                last.then_inc(to_stat, 1)

            def scalars_out(job):
                ws = XJOBS[job]
                product_done(job, 2)
                n = len(ws) * 2 * CHUNKS
                nc.vector.tensor_copy(scal[:, ws.start:ws.stop, :, :].rearrange("p w k c -> p (w k c)"),
                                      ps_stat[:, 0:n]).then_inc(stat_read, 1)

            def b_out(g):
                dve.wait_ge(b_done, g + 1)
                if g >= 2:
                    dve.wait_ge(ab_done, g - 1)
                nc.vector.tensor_tensor(
                    bsb[:, g % 2, :, :].rearrange("p c (t l) -> p (c t) l", t=2),
                    ps_b[:].rearrange("p (n l) -> p n l", l=D),
                    bb.broadcast_to([128, GP, D]), ALU.add).then_inc(bsb_ready, 1)

            def z_out(g):
                dve.wait_ge(gate_ready, g + 1)
                dve.wait_ge(ab_done, g + 1)
                nc.vector.tensor_tensor(
                    zt[:, g // 2, :, 64 * (g % 2):64 * (g % 2 + 1)].rearrange("p r n -> p n r"),
                    ps_ab[:].rearrange("p (n r) -> p n r", r=ROWS),
                    gate[:, g % 2, :].rearrange("p (n r) -> p n r", r=ROWS), ALU.mult).then_inc(zt_ready, 1)

            def x1_out(w, n):
                dve.wait_ge(o_done, 2 * w + n + 1)
                if n == 0:
                    dve.wait_ge(xb_ready, 2 * w + 2)
                rows = slice(n * ROWS // 2, (n + 1) * ROWS // 2)
                nc.vector.tensor_tensor(
                    x1[:, w, :, rows, :].rearrange("p n r d -> p r n d"),
                    ps_o[:, 512 * n:512 * n + 512].rearrange("p (r n d) -> p r n d", n=2, d=D),
                    xb[:, w, :, rows, :].rearrange("p n r d -> p r n d"), ALU.add).then_inc(x1_ready, 1)

            def x1_stats(w, n, p2):
                if p2 == 0:
                    dve.wait_ge(x1_ready, 2 * w + n + 1)
                last = nc.vector.bn_stats(
                    part[:, 1, w, p2, n, :],
                    x1[:, w, p2, n * ROWS // 2:(n + 1) * ROWS // 2, :].rearrange("p r d -> p (r d)"))
                if n == 1 and p2 == 1:
                    link(last)
                    partition_stats(1, range(w, w + 1), 2)

            def x1_mean(w):
                group_stats(X1JOB + w, 1, range(w, w + 1))
                link(nc.vector.tensor_scalar(pad[:, w, :], mean[:, 1, w, :], last_block, None, ALU.mult))
                dve.wait_ge(row_done, w + 1)
                nc.vector.tensor_tensor(
                    x1[:, w, :, ROWS, :], ps_row.rearrange("p (n d) -> p n d", d=D),
                    pad[:, w, :].rearrange("p (n o) -> p n o", o=1).broadcast_to([128, 2, D]),
                    ALU.add).then_inc(row_ready, 1)

            def x1_variance(w):
                group_variance(X1JOB + w, 1, range(w, w + 1))

            def filter_coefs(w):
                minus_mean_rstd(X1JOB + w, 1, range(w, w + 1))
                h = w % 2
                for k, cols in ((1, slice(4, 6)), (0, slice(0, 4))):
                    n = cols.stop - cols.start
                    last = nc.vector.tensor_tensor(
                        coef[:, w, :, cols], own_taps[:, h, :, cols],
                        norm[:, 1, w, k, :].rearrange("p (n o) -> p n o", o=1).broadcast_to([128, 2, n]), ALU.mult)
                link(last)
                nc.vector.tensor_scalar_add(coef[:, w, :, 0:1], coef[:, w, :, 0:1], 1.0).then_inc(coef_ready, 1)

            def filter_rest(w, p2, k):
                dve.wait_ge(y_pool, 2 * w + p2 + 1)
                yw = y[:, w, p2, :, :]
                if k == 0:
                    left = yw[:, :, 0:D - 1]
                    link(nc.vector.scalar_tensor_tensor(left, x1[:, w, p2, 0:ROWS, 1:D], coef[:, w, p2, 1:2], left,
                                                        ALU.mult, ALU.add))
                else:
                    nc.vector.scalar_tensor_tensor(yw, x1[:, w, p2, 1:ROWS + 1, :], coef[:, w, p2, 2:3], yw, ALU.mult,
                                                   ALU.add).then_inc(y_dve, 1)

            def last_taps():
                w = WAVES - 1
                yw, f = y[:, w, 0, :, :], own_taps[:, w % 2, 0, :]
                left, edge = yw[:, :, 0:D - 1], yw[:, :, D - 1:D]
                here, below = x1[:, w, 0, 0:ROWS, :], x1[:, w, 0, 1:ROWS + 1, :]
                dve.wait_ge(last_base, 1)
                nc.vector.tensor_scalar(edge, edge, offs[:, 0, 1:2], None, ALU.add)
                link(nc.vector.scalar_tensor_tensor(left, here[:, :, 1:D], f[:, 1:2], left, ALU.mult, ALU.add))
                link(nc.vector.scalar_tensor_tensor(yw, below, f[:, 2:3], yw, ALU.mult, ALU.add))
                link(nc.vector.scalar_tensor_tensor(left, below[:, :, 1:D], f[:, 3:4], left, ALU.mult, ALU.add))

            def last_filter(p2):
                w = WAVES - 1
                yw = y[:, w, p2, :, :]
                dve.wait_ge(rstd_done, X1JOB + w + 1)
                nc.vector.scalar_tensor_tensor(yw, yw, norm[:, 1, w, 0, p2:p2 + 1], x1[:, w, p2, 0:ROWS, :],
                                               ALU.mult, ALU.add).then_inc(y_dve, 1)

            nc.vector.memset(zeros[:], 0.0).then_inc(zeros_set, 1)
            for r in range(2):
                nc.vector.memset(abd[0:64, r, :, :, 1, :], 0.0)
                last = nc.vector.memset(abd[64:128, r, :, :, 0, :], 0.0)
            last.then_inc(abd_zeroed, 1)
            x_stats(0)
            partition_stats(0, XJOBS[0], 1)
            group_stats(0, 0, XJOBS[0])
            dve.wait_ge(masks_in, 16)
            x_shares(0)
            group_variance(0, 0, XJOBS[0])
            dve.wait_ge(params_in, 16)
            taps = own_taps[:].rearrange("p h n k -> p (h n) k")
            nc.vector.tensor_copy(taps[:, :, 0:4].rearrange("p n (a b) -> p n a b", b=2), ftap[:, :, 1:4:2, 1:4:2])
            nc.vector.tensor_reduce(taps[:, :, 4], ftap[:, :, 1:4:2, 1:4:2], mybir.AxisListType.XY, ALU.add)
            link(nc.vector.tensor_reduce(taps[:, :, 5], ftap[:, :, 1:4:2, 3:4], mybir.AxisListType.XY, ALU.add))
            nc.vector.tensor_scalar(taps[:, :, 5:6], taps[:, :, 5:6], -1.0, None, ALU.mult).then_inc(taps_ready, 1)
            dve.wait_ge(taps_ready, 1)
            x_scalars(0)
            scalars_out(0)
            dve.wait_ge(stat_read, nth(0, 2))
            dve.wait_ge(t_done, 1)
            for c in DVE0:
                last = nc.vector.tensor_scalar(rt[:, 0, c * 128:c * 128 + 128], ps_ab[:, c * 128:c * 128 + 128],
                                               scalar_of(0, c, 0), scalar_of(0, c, 1), ALU.mult, ALU.add)
            last.then_inc(rt0_dve, 1)
            x_stats(1)
            partition_stats(0, XJOBS[1], 1)
            for g in range(GROUPS):
                if g == 0:
                    group_stats(1, 0, XJOBS[1])
                elif g == 1:
                    scalars_out(1)
                elif g == 2:
                    group_stats(2, 0, XJOBS[2])
                    x_shares(2)
                elif g == 3:
                    scalars_out(2)
                w = g // 2 - 1
                if g >= 2 and g % 2 == 0:
                    x1_out(w, 0)
                    x1_stats(w, 0, 0)
                    x1_stats(w, 0, 1)
                elif g >= 2:
                    x1_mean(w)
                b_out(g)
                if g == 0:
                    group_variance(1, 0, XJOBS[1])
                    x_shares(1)
                    x_stats(2)
                    x_scalars(1)
                    x_stats(3)
                elif g == 1:
                    partition_stats(0, XJOBS[2], 1)
                elif g == 2:
                    group_variance(2, 0, XJOBS[2])
                if g >= 2 and g % 2 == 0:
                    x1_out(w, 1)
                    if g == 2:
                        x_scalars(2)
                    x1_stats(w, 1, 0)
                    x1_stats(w, 1, 1)
                elif g >= 2:
                    x1_variance(w)
                    if w >= 1:
                        filter_rest(w - 1, 0, 1)
                    filter_coefs(w)
                z_out(g)
                if g >= 2 and g % 2 == 1 and w >= 1:
                    filter_rest(w - 1, 1, 0)
                    filter_rest(w - 1, 1, 1)
            last = WAVES - 1
            x1_out(last, 0)
            x1_stats(last, 0, 0)
            x1_out(last, 1)
            x1_stats(last, 0, 1)
            x1_stats(last, 1, 0)
            x1_stats(last, 1, 1)
            x1_mean(last)
            x1_variance(last)
            dve.wait_ge(offs_ready, 1)
            last_taps()
            last_filter(0)
            dve.wait_ge(last_sum_ready, 1)
            edge = y[:, last, 1, :, D - 1:D]
            link(nc.vector.tensor_scalar(edge, edge, offs[:, 1, 1:2], None, ALU.add))
            last_filter(1)

        @block.tensor
        def _(pe):
            def idle_products(n):
                for _ in range(n):
                    nc.tensor.matmul(ps_g[:, 0:128], zeros[:],
                                     zeros[:], start=True, stop=True)

            def stat_product(job, step):
                pe.wait_ge(to_stat, nth(job, step))
                if nth(job, step) > 1:
                    pe.wait_ge(stat_read, nth(job, step) - 1)
                ws = XJOBS[job] if job < X1JOB else range(job - X1JOB, job - X1JOB + 1)
                k, s, n = int(job >= X1JOB), slice(ws.start, ws.stop), 2 * len(ws)
                if step < 2:
                    operand = mv[:, k, s, :, 0] if step == 0 else second[:, k, s, :]
                    nc.tensor.matmul(ps_stat[:, 0:n], average, operand, start=True, stop=True).then_inc(stat_done, 1)
                else:
                    for p2 in range(2):
                        last = nc.tensor.matmul(ps_stat[64 * p2:64 * p2 + 64, 0:n * CHUNKS], spread,
                                                sel[:, p2, s, :, :].rearrange("p w k c -> p (w k c)"),
                                                start=True, stop=True)
                    last.then_inc(stat_done, 1)

            def transposes(g):
                pe.wait_ge(nat_in[g], 16)
                if g >= 1:
                    pe.wait_ge(rt_ready, g)
                for c in range(CH):
                    p = g * GP + 2 * c
                    ps = ps_ab if g == 0 and c in DVE0 else ps_t
                    last = nc.tensor.transpose(ps[:, c * 128:(c + 1) * 128],
                                               xnat[:, p:p + 2, :].rearrange("p n d -> p (n d)"), ident)
                last.then_inc(t_done, 1)

            def product_a(g):
                if g == 0:
                    pe.wait_ge(rt0_dve, 1)
                pe.wait_ge(rt_ready, g + 1)
                if g >= 1:
                    pe.wait_ge(abd_ready, g)
                nc.tensor.matmul(ps_a[:], W_A, rt[:, g, :], start=True, stop=True).then_inc(a_done, 1)

            def product_b(g):
                if g >= 1:
                    pe.wait_ge(bsb_ready, g)
                for c in range(CH):
                    last = nc.tensor.matmul(ps_b[:, c * 128:(c + 1) * 128], rt[:, g, c * 128:(c + 1) * 128], W_B,
                                            start=True, stop=True)
                last.then_inc(b_done, 1)

            def product_g(g):
                if g >= 1:
                    pe.wait_ge(gate_ready, g)
                nc.tensor.matmul(ps_g[:], W_G, rt[:, g, :], start=True, stop=True).then_inc(g_done, 1)

            def product_ab(g):
                pe.wait_ge(abd_ready, g + 1)
                pe.wait_ge(bsb_ready, g + 1)
                if g >= 1:
                    pe.wait_ge(zt_ready, g)
                for c in range(CH):
                    for p2 in range(2):
                        last = nc.tensor.matmul(
                            ps_ab[64 * p2:64 * p2 + 64, c * 128:(c + 1) * 128],
                            bsb[:, g % 2, c, 64 * p2:64 * p2 + 64],
                            abd[:, g % 2, c, p2, :, :].rearrange("p t j -> p (t j)"), start=True, stop=True)
                last.then_inc(ab_done, 1)

            def product_o(w, n):
                pe.wait_ge(zt_ready, 2 * w + 2)
                if w >= 1:
                    pe.wait_ge(row_ready, w)
                for r in range(n * ROWS // 2, (n + 1) * ROWS // 2):
                    last = nc.tensor.matmul(ps_o[:, r * 128:(r + 1) * 128],
                                            zt[:, w, r, :], W_O, start=True, stop=True)
                last.then_inc(o_done, 1)

            def rows_below(w):
                pe.wait_ge(x1_ready, 2 * w + 2)
                nc.tensor.matmul(ps_row, above, x1[:, w, :, 0, :], start=True, stop=True).then_inc(row_done, 1)

            def last_sum(n):
                w = WAVES - 1
                if n == 0:
                    pe.wait_ge(diag_ready, 1)
                    pe.wait_ge(abd_ready, GROUPS)
                else:
                    pe.wait_ge(row_ready, w + 1)
                rows = x1[:, w, 1, n:n + ROWS, :]
                nc.tensor.matmul(ps_a[:], diag[:, 2 * n, :], rows.rearrange("p r d -> p (r d)"),
                                 start=(n == 0), stop=False)
                if n == 0:
                    stat_product(X1JOB + w, 0)
                ins = nc.tensor.matmul(ps_a[:].rearrange("p (r d) -> p r d", d=D)[:, :, 0:D - 1],
                                       diag[:, 2 * n + 1, :], rows[:, :, 1:D], start=False, stop=(n == 1))
                if n == 1:
                    ins.then_inc(sum_pe, 1)

            pe.wait_ge(zeros_set, 1)
            idle_products(WARM[0])
            pe.wait_ge(masks_in, 16)
            stat_product(0, 0)
            idle_products(WARM[1])
            stat_product(0, 1)
            transposes(0)
            idle_products(WARM[2])
            stat_product(0, 2)
            idle_products(WARM[3])
            pe.wait_ge(params_in, 16)
            for g in range(GROUPS):
                w = g // 2 - 1
                product_a(g)
                if g + 1 < GROUPS:
                    transposes(g + 1)
                if g == 0:
                    stat_product(1, 0)
                elif g == 1:
                    stat_product(1, 2)
                elif g == 2:
                    stat_product(2, 0)
                elif g == 3:
                    stat_product(2, 2)
                if g >= 2 and g % 2 == 0:
                    product_o(w, 0)
                elif g >= 2:
                    rows_below(w)
                    stat_product(X1JOB + w, 0)
                product_b(g)
                if g == 0:
                    stat_product(1, 1)
                elif g == 2:
                    stat_product(2, 1)
                if g >= 2 and g % 2 == 0:
                    product_o(w, 1)
                elif g >= 2:
                    stat_product(X1JOB + w, 1)
                product_g(g)
                product_ab(g)
            last = WAVES - 1
            for n in range(2):
                product_o(last, n)
            rows_below(last)
            last_sum(0)
            stat_product(X1JOB + last, 1)
            last_sum(1)


def kernel(x, L0_conv_Wa, L0_conv_ba, L0_conv_Wb, L0_conv_bb, L0_conv_Wg, L0_conv_bg, L0_conv_Wo, L0_conv_bo,
           L1_conv_filt):
    import concourse.bacc as _bacc
    from concourse.bass_utils import run_bass_kernel_spmd as _run

    given = [np.asarray(a) for a in (L0_conv_Wa, L0_conv_ba, L0_conv_Wb, L0_conv_bb, L0_conv_Wg, L0_conv_bg,
                                     L0_conv_Wo, L0_conv_bo, L1_conv_filt)]
    arrays = {
        "x": np.ascontiguousarray(x),
        "params": np.ascontiguousarray(np.concatenate(mask_columns() + parameter_columns(*given), axis=1)),
    }
    nc = _bacc.Bacc("TRN2", target_bir_lowering=False, num_devices=1)
    args = [nc.dram_tensor(n, a.shape, mybir.dt.from_np(a.dtype), kind="ExternalInput").ap()
            for n, a in arrays.items()]
    out = nc.dram_tensor("out", arrays["x"].shape, mybir.dt.float32, kind="ExternalOutput").ap()
    preact_pair_mix_blur(nc, *args, out)
    return _run(nc, [arrays], core_ids=[0]).results[0]["out"]
```

```python
import numpy as np

import concourse.bass as bass
from concourse import mybir
from contextlib import ExitStack

BLOCKS = 8
ROWS = 8
CHUNKS = 8
TAPS = 16


def mask_columns():
    p = np.arange(128)
    chunk = p // 16
    average = (chunk[:, None] == chunk[None, :]) / 16.0
    spread = np.full((128, 64), 1 / 16.0)
    select = chunk[:, None] == np.arange(CHUNKS)[None, :]
    last = p % BLOCKS == BLOCKS - 1
    above = (p[:, None] == p[None, :] + 1) & ~last[None, :]
    return [m.astype(np.float32) for m in (average, spread, select, np.eye(128), above, last[:, None])]


def parameter_columns(Wa, ba, Wb, bb, Wg, bg, Wo, bo, filt):
    weights = np.zeros((128, 4, 128), np.float32)
    for n, m in enumerate((Wa, Wg, Wb, Wo)):
        weights[:64, n, :64] = m
        weights[64:, n, 64:] = m
    cols = np.tile(np.stack([ba, bg], axis=1), (2, 1))
    rows = np.tile(np.concatenate([bb, bo])[None, :], (128, 1))
    taps = filt.reshape(2, CHUNKS, 2, 2, TAPS).transpose(1, 3, 0, 2, 4).reshape(16, 4 * TAPS)
    return [weights.reshape(128, 512), cols, rows, np.repeat(taps, BLOCKS, axis=0)]


def preact_pair_mix_blur(nc, x, params, out):
    fp32 = mybir.dt.float32
    ALU = mybir.AluOpType
    ACT = mybir.ActivationFunctionType

    B, C, H, D = x.shape
    WP = 2 * CHUNKS
    PAIRS = B * C // 2
    WAVES = PAIRS // WP
    CH = CHUNKS // 2
    GP = 2 * CH
    GROUPS = PAIRS // GP
    EPS = 1e-5

    x_nat = x.rearrange("b (g t) j d -> (t j) (b g) d", t=2)

    def slab_view(t, w, p2):
        b, h = divmod(w, WAVES // B)
        return t[b, h * 2 * WP:(h + 1) * 2 * WP, :, :].rearrange(
            "(c p t) (q r) d -> p c (t q) (r d)", p=2, t=2, q=BLOCKS)[p2]

    ctx = ExitStack()
    with ctx:
        def sb(name, shape):
            return ctx.enter_context(nc.sbuf_tensor(name, shape, fp32))

        def pb(name, shape):
            return ctx.enter_context(nc.psum_tensor(name, shape, fp32))

        def sem(name):
            return ctx.enter_context(nc.semaphore(name))

        par = sb("par", [128, params.shape[1]])
        ends = np.cumsum([0, 128, 64, CHUNKS, 128, 128, 1, 4 * 128, 2, 2 * D, 4 * TAPS]).tolist()
        average, spread, select, ident, above, last_block, wbd, bcol, brow, ftap = (
            par[:, a:b] for a, b in zip(ends, ends[1:]))
        MASKS = ends[6]
        W_A, W_G, W_B, W_O = (wbd[:, 128 * n:128 * n + 128] for n in range(4))
        bb = brow[:, 0:D].rearrange("p (n d) -> p n d", n=1)
        bo = brow[:, D:2 * D].rearrange("p (n d) -> p n d", n=1)
        ftap = ftap.rearrange("p (n a b) -> p n a b", a=4, b=4)
        own_taps = sb("own_taps", [128, 2, 2, 6])
        xs = sb("xs", [128, WAVES, 2, ROWS, D])
        xnat = sb("xnat", [128, PAIRS, D])
        xb = sb("xb", [128, WAVES, 2, ROWS, D])
        rt = sb("rt", [128, GROUPS, CH * 128])
        abd = sb("abd", [128, 2, CH, 2, 2, 64])
        bsb = sb("bsb", [128, 2, CH, 128])
        gate = sb("gate", [128, 2, CH * 128])
        zt = sb("zt", [128, WAVES, ROWS, 128])
        x1 = sb("x1", [128, WAVES, 2, ROWS + 1, D])
        y = sb("y", [128, WAVES, 2, ROWS, D])
        prod = sb("prod", [128, WAVES - 1, 2, 3, ROWS, D])
        last_below = sb("last_below", [128, ROWS, D])
        part = sb("part", [128, 2, WAVES, 2, 2, 6])
        mv = sb("mv", [128, 2, WAVES, 2, 2])
        mean = sb("mean", [128, 2, WAVES, 2])
        dev = sb("dev", [128, 2, WAVES, 2])
        second = sb("second", [128, 2, WAVES, 2])
        veps = sb("veps", [128, 2, WAVES, 2])
        norm = sb("norm", [128, 2, WAVES, 2, 2])
        sel = sb("sel", [128, 2, WAVES, 2, CHUNKS])
        share = sb("share", [128, 2, WAVES, 2, CHUNKS])
        scal = sb("scal", [128, WAVES, 2, CHUNKS])
        coef = sb("coef", [128, WAVES, 2, 6])
        pad = sb("pad", [128, WAVES, 2])
        offs = sb("offs", [128, 2, 2])
        diag = sb("diag", [128, TAPS // 4, 128])
        half = sb("half", [128, 2 * WAVES])
        warm = sb("warm", [128, 1])
        zeros = sb("zeros", [128, 128])

        ps_t = pb("ps_t", [128, 512])
        ps_a = pb("ps_a", [128, 512])
        ps_b = pb("ps_b", [128, 512])
        ps_g = pb("ps_g", [128, 512])
        ps_ab = pb("ps_ab", [128, 512])
        ps_o = pb("ps_o", [128, 1024])
        ps_s = pb("ps_s", [128, 512])
        ps_stat = ps_s[:, 0:128]
        ps_row = ps_o[:, 0:128]

        masks_in, params_in = sem("masks_in"), sem("params_in")
        xs_in = [[sem(f"xs_in{w}_{p2}") for p2 in range(2)] for w in range(WAVES)]
        nat_in = [sem(f"nat_in{g}") for g in range(GROUPS)]
        stored = sem("stored")
        half_set, abd_zeroed = sem("half_set"), sem("abd_zeroed")
        zeros_set = sem("zeros_set")
        dve_step = sem("dve_step")
        to_stat, stat_done = sem("to_stat"), sem("stat_done")
        stat_read = sem("stat_read")
        rstd_done = sem("rstd_done")
        taps_ready, diag_ready = sem("taps_ready"), sem("diag_ready")
        xb_ready = sem("xb_ready")
        t_done, rt_ready, rt0_dve = sem("t_done"), sem("rt_ready"), sem("rt0_dve")
        a_done, abd_ready = sem("a_done"), sem("abd_ready")
        b_done, bsb_ready = sem("b_done"), sem("bsb_ready")
        g_done, gate_ready = sem("g_done"), sem("gate_ready")
        ab_done, zt_ready = sem("ab_done"), sem("zt_ready")
        o_done, x1_ready = sem("o_done"), sem("x1_ready")
        row_done, row_ready = sem("row_done"), sem("row_ready")
        coef_ready, base_ready = sem("coef_ready"), sem("base_ready")
        pool_step = sem("pool_step")
        y_pool, y_dve = sem("y_pool"), sem("y_dve")
        prod_ready = sem("prod_ready")
        edge_ready, right_ready = sem("edge_ready"), sem("right_ready")
        offs_ready, last_base = sem("offs_ready"), sem("last_base")
        sum_pe, last_sum_ready = sem("sum_pe"), sem("last_sum_ready")

        block = ctx.enter_context(nc.Block())

        XJOBS = [range(0, 1), range(1, 2), range(2, WAVES)]
        X1JOB = len(XJOBS)
        STATS = [(0, 0), (0, 1), (0, 2), (1, 0), (1, 1), (1, 2), (2, 0), (2, 1), (2, 2)]
        STATS += [(X1JOB + w, step) for w in range(WAVES) for step in range(2)]

        def nth(job, step):
            return STATS.index((job, step)) + 1

        IDLE = (8, 2, 0, 3)
        DVE0 = range(2, 4)

        def scalar_of(g, c, k):
            n = CH * (g % 2) + c
            return scal[:, g // 2, k, n:n + 1]

        @block.sync
        def _(sp):
            def load_slab(w):
                for p2 in range(2):
                    sp.dma_start(xs[:, w, p2, :, :].rearrange("p r d -> p (r d)"),
                                 slab_view(x, w, p2)).then_inc(xs_in[w][p2], 16)

            def load_nat(g):
                sp.dma_start(xnat[:, g * GP:(g + 1) * GP, :],
                             x_nat[:, g * GP:(g + 1) * GP, :]).then_inc(nat_in[g], 16)

            load_slab(0)
            sp.dma_start(par[:, 0:MASKS], params[:, 0:MASKS]).then_inc(masks_in, 16)
            load_nat(0)
            load_nat(1)
            sp.dma_start(par[:, MASKS:], params[:, MASKS:]).then_inc(params_in, 16)
            load_slab(1)
            load_nat(2)
            load_slab(2)
            load_slab(3)
            for g in range(3, GROUPS):
                load_nat(g)
            for w, p2 in [(w, p2) for w in range(WAVES) for p2 in range(2)]:
                if w == WAVES - 2 or (w < WAVES - 2 and p2 == 1):
                    sp.wait_ge(y_pool, 2 * w + p2 + 1)
                else:
                    sp.wait_ge(y_dve, w + 1 if p2 == 0 and w < WAVES - 1 else WAVES - 1 + p2)
                sp.dma_start(slab_view(out, w, p2),
                             y[:, w, p2, :, :].rearrange("p r d -> p (r d)")).then_inc(stored, 16)
            sp.wait_ge(stored, 16 * 2 * WAVES)

        @block.gpsimd
        def _(pool):
            nc.gpsimd.memset(half[:], -0.5).then_inc(half_set, 1)
            pool.wait_ge(half_set, 1)

            def inverse_root(job, k, ws):
                pool.wait_ge(stat_read, nth(job, 1))
                v = veps[:, k, ws.start:ws.stop, :].rearrange("p w n -> p (w n)")
                nc.gpsimd.tensor_tensor(norm[:, k, ws.start:ws.stop, 0, :], v.rearrange("p (w n) -> p w n", n=2),
                                        half[:, 0:2 * len(ws)].rearrange("p (w n) -> p w n", n=2),
                                        ALU.pow).then_inc(rstd_done, 1)

            def x1_inverse_root(w):
                inverse_root(X1JOB + w, 1, range(w, w + 1))

            def add_bo(w):
                for p2 in range(2):
                    pool.wait_ge(xs_in[w][p2], 16)
                    nc.gpsimd.tensor_tensor(xb[:, w, p2, :, :], xs[:, w, p2, :, :],
                                            bo.broadcast_to([128, ROWS, D]), ALU.add).then_inc(xb_ready, 1)

            own_steps = [0]

            def link(ins):
                own_steps[0] += 1
                ins.then_inc(pool_step, 1)
                pool.wait_ge(pool_step, own_steps[0])

            def right_product(w):
                pool.wait_ge(coef_ready, w + 1)
                link(nc.gpsimd.tensor_scalar(prod[:, w, 0, 0, :, 0:D - 1], x1[:, w, 0, 0:ROWS, 1:D],
                                             coef[:, w, 0, 1:2], None, ALU.mult))

            def edge_correction(w, p2):
                pool.wait_ge(base_ready, 2 * w + p2 + 1)
                edge = y[:, w, p2, :, D - 1:D]
                nc.gpsimd.tensor_scalar(edge, edge, coef[:, w, p2, 5:6], None, ALU.add)

            def add_product(w, p2, k, n):
                if n:
                    pool.wait_ge(prod_ready, n)
                cols = slice(0, D - (k + 1) % 2)
                y_w = y[:, w, p2, :, cols]
                return nc.gpsimd.tensor_tensor(y_w, y_w, prod[:, w, p2, k, :, cols], ALU.add)

            inverse_root(0, 0, XJOBS[0])
            pool.wait_ge(params_in, 16)
            add_bo(0)
            inverse_root(1, 0, XJOBS[1])
            add_bo(1)
            add_bo(2)
            pool.wait_ge(taps_ready, 1)
            for n in range(TAPS // 4):
                last = nc.gpsimd.tensor_scalar(diag[:, n, :], ident, own_taps[:, (WAVES - 1) % 2, 1, n:n + 1], None,
                                               ALU.mult)
            last.then_inc(diag_ready, 1)
            inverse_root(2, 0, XJOBS[2])
            add_bo(3)
            x1_inverse_root(0)
            for w in range(WAVES - 2):
                right_product(w)
                edge_correction(w, 0)
                link(add_product(w, 0, 0, None))
                add_product(w, 0, 2, 3 * w + 1).then_inc(y_pool, 1)
                edge_correction(w, 1)
                pool.wait_ge(right_ready, w + 1)
                link(add_product(w, 1, 2, 3 * w + 2))
                x1_inverse_root(w + 1)
                add_product(w, 1, 1, 3 * w + 3).then_inc(y_pool, 1)
            w, n = WAVES - 2, 3 * (WAVES - 2)
            pool.wait_ge(edge_ready, 1)
            pool.wait_ge(right_ready, w + 1)
            link(add_product(w, 0, 1, n + 1))
            add_product(w, 0, 2, n + 2).then_inc(y_pool, 1)
            pool.wait_ge(base_ready, 2 * w + 2)
            link(add_product(w, 1, 0, n + 3))
            pool.wait_ge(edge_ready, 2)
            link(add_product(w, 1, 1, n + 4))
            x1_inverse_root(WAVES - 1)
            add_product(w, 1, 2, n + 5).then_inc(y_pool, 1)

        @block.scalar
        def _(act):
            act.wait_ge(half_set, 1)
            nc.scalar.activation(warm[:], half[:, 0:1], ACT.Sigmoid)

            def transposed_out(g):
                act.wait_ge(t_done, g + 1)
                job = min(g // 2, 2)
                act.wait_ge(stat_read, nth(job, 2))
                chunks = range(CH) if g > 0 else range(DVE0.start)
                ps = ps_o if g == 1 else ps_t
                for c in chunks:
                    n = slice(c * 128, c * 128 + 128)
                    last = nc.scalar.activation(rt[:, g, n], ps[:, n], ACT.Identity,
                                                bias=scalar_of(g, c, 1), scale=scalar_of(g, c, 0))
                last.then_inc(rt_ready, 1)

            def a_out(g):
                act.wait_ge(a_done, g + 1)
                if g >= 2:
                    act.wait_ge(ab_done, g - 1)
                src = ps_a[:].rearrange("p (c t j) -> p c t j", c=CH, t=2)
                for p2 in range(2):
                    for i2 in range(2):
                        last = nc.scalar.activation(
                            abd[64 * i2:64 * i2 + 64, g % 2, :, p2, i2, :],
                            src[64 * p2:64 * p2 + 64, :, i2, :], ACT.Identity,
                            bias=bcol[64 * p2:64 * p2 + 64, 0:1])
                last.then_inc(abd_ready, 1)

            def gate_out(g):
                act.wait_ge(g_done, g + 1)
                if g >= 2:
                    act.wait_ge(zt_ready, g - 1)
                nc.scalar.activation(gate[:, g % 2, :], ps_g[:], ACT.Sigmoid,
                                     bias=bcol[:, 1:2]).then_inc(gate_ready, 1)

            def filter_base(w, p2):
                act.wait_ge(coef_ready, w + 1)
                nc.scalar.activation(y[:, w, p2, :, :], x1[:, w, p2, 0:ROWS, :], ACT.Identity,
                                     bias=coef[:, w, p2, 4:5], scale=coef[:, w, p2, 0:1]).then_inc(base_ready, 1)

            def filter_product(w, p2, k):
                row, col = (k + 1) // 2, (k + 1) % 2
                act.wait_ge(row_ready, w + 1)
                nc.scalar.activation(prod[:, w, p2, k, :, 0:D - col], x1[:, w, p2, row:row + ROWS, col:D], ACT.Copy,
                                     scale=coef[:, w, p2, k + 1:k + 2]).then_inc(prod_ready, 1)

            transposed_out(0)
            act.wait_ge(params_in, 16)
            act.wait_ge(abd_zeroed, 1)
            for g in range(GROUPS):
                a_out(g)
                if g + 1 < GROUPS:
                    transposed_out(g + 1)
                if g % 2 == 0 and g >= 4:
                    for p2 in range(2):
                        filter_base(g // 2 - 2, p2)
                gate_out(g)
                if g % 2 == 0 and g >= 4:
                    for p2 in range(2):
                        filter_product(g // 2 - 2, p2, 2)
                elif g >= 4:
                    filter_product(g // 2 - 2, 1, 1)
            w = WAVES - 2
            filter_base(w, 0)
            filter_product(w, 0, 1)
            filter_product(w, 0, 2)
            filter_base(w, 1)
            filter_product(w, 1, 0)
            last = WAVES - 1
            act.wait_ge(x1_ready, 2 * WAVES)
            nc.scalar.activation(y[:, last, 0, :, :], x1[:, last, 0, 0:ROWS, :], ACT.Copy,
                                 scale=own_taps[:, last % 2, 0, 0:1]).then_inc(last_base, 1)
            filter_product(w, 1, 1)
            filter_product(w, 1, 2)
            act.wait_ge(offs_ready, 1)
            act.wait_ge(row_ready, WAVES)
            nc.scalar.activation(last_below[:], x1[:, last, 0, 1:ROWS + 1, :], ACT.Identity,
                                 bias=offs[:, 0, 0:1], scale=own_taps[:, last % 2, 0, 2:3]).then_inc(last_base, 1)
            act.wait_ge(sum_pe, 1)
            nc.scalar.activation(y[:, last, 1, :, :], ps_a[:].rearrange("p (r d) -> p r d", d=D), ACT.Identity,
                                 bias=offs[:, 1, 0:1]).then_inc(last_sum_ready, 1)

        @block.vector
        def _(dve):
            steps = [0]

            def link(ins):
                steps[0] += 1
                ins.then_inc(dve_step, 1)
                dve.wait_ge(dve_step, steps[0])

            def product_done(job, step):
                dve.wait_ge(stat_done, nth(job, step))

            def partition_stats(k, ws, halves):
                for w in ws:
                    for p2 in range(2):
                        last = nc.vector.bn_aggr(
                            mv[:, k, w, p2, :], part[:, k, w, p2, 0:halves, :].rearrange("p a b -> p (a b)"))
                last.then_inc(to_stat, 1)

            def group_stats(job, k, ws):
                s = slice(ws.start, ws.stop)
                n = 2 * len(ws)
                ps = ps_stat[:, 0:n].rearrange("p (w n) -> p w n", n=2)
                product_done(job, 0)
                nc.vector.tensor_copy(mean[:, k, s, :], ps).then_inc(stat_read, 1)
                dve.wait_ge(stat_read, nth(job, 0))
                if job == X1JOB + WAVES - 1:
                    nc.vector.scalar_tensor_tensor(
                        offs[:], mean[:, 1, WAVES - 1, :].rearrange("p (n o) -> p n o", o=1).broadcast_to([128, 2, 2]),
                        -1.0, own_taps[:, (WAVES - 1) % 2, :, 4:6], ALU.mult, ALU.mult).then_inc(offs_ready, 1)
                link(nc.vector.tensor_tensor(dev[:, k, s, :], mv[:, k, s, :, 0], mean[:, k, s, :], ALU.subtract))
                link(nc.vector.tensor_tensor(dev[:, k, s, :], dev[:, k, s, :], dev[:, k, s, :], ALU.mult))
                nc.vector.tensor_tensor(second[:, k, s, :], dev[:, k, s, :], mv[:, k, s, :, 1],
                                        ALU.add).then_inc(to_stat, 1)

            def group_variance(job, k, ws):
                s = slice(ws.start, ws.stop)
                product_done(job, 1)
                nc.vector.tensor_scalar_add(veps[:, k, s, :],
                                            ps_stat[:, 0:2 * len(ws)].rearrange("p (w n) -> p w n", n=2),
                                            EPS).then_inc(stat_read, 1)

            def minus_mean_rstd(job, k, ws):
                s = slice(ws.start, ws.stop)
                dve.wait_ge(rstd_done, job + 1)
                link(nc.vector.scalar_tensor_tensor(norm[:, k, s, 1, :], mean[:, k, s, :], -1.0, norm[:, k, s, 0, :],
                                                    ALU.mult, ALU.mult))

            def x_stats(w, p2s=(0, 1)):
                for p2 in p2s:
                    dve.wait_ge(xs_in[w][p2], 16)
                    last = nc.vector.bn_stats(part[:, 0, w, p2, 0, :], xs[:, w, p2, :, :].rearrange("p r d -> p (r d)"))
                if 1 in p2s:
                    link(last)

            def x_shares(job):
                for p2 in range(2):
                    for w in XJOBS[job]:
                        nc.vector.tensor_copy(share[:, p2, w, 0, :], select)
                        last = nc.vector.tensor_scalar(share[:, p2, w, 1, :], select, mean[:, 0, w, p2:p2 + 1], -1.0,
                                                       ALU.mult, ALU.mult)
                link(last)

            def x_scalars(job):
                ws = XJOBS[job]
                dve.wait_ge(rstd_done, job + 1)
                for w in ws:
                    last = nc.vector.tensor_tensor(
                        sel[:, :, w, :, :].rearrange("p n k c -> p n (k c)"),
                        share[:, :, w, :, :].rearrange("p n k c -> p n (k c)"),
                        norm[:, 0, w, 0, :].rearrange("p (n o) -> p n o", o=1).broadcast_to([128, 2, 2 * CHUNKS]),
                        ALU.mult)
                last.then_inc(to_stat, 1)

            def scalars_out(job):
                ws = XJOBS[job]
                product_done(job, 2)
                n = len(ws) * 2 * CHUNKS
                nc.vector.tensor_copy(scal[:, ws.start:ws.stop, :, :].rearrange("p w k c -> p (w k c)"),
                                      ps_stat[:, 0:n]).then_inc(stat_read, 1)

            def b_out(g):
                dve.wait_ge(b_done, g + 1)
                if g >= 2:
                    dve.wait_ge(ab_done, g - 1)
                nc.vector.tensor_tensor(
                    bsb[:, g % 2, :, :].rearrange("p c (t l) -> p (c t) l", t=2),
                    ps_b[:].rearrange("p (n l) -> p n l", l=D),
                    bb.broadcast_to([128, GP, D]), ALU.add).then_inc(bsb_ready, 1)

            def z_out(g, parts=1):
                dve.wait_ge(gate_ready, g + 1)
                dve.wait_ge(ab_done, g + 1)
                for n in range(parts):
                    rows = slice(n * ROWS // parts, (n + 1) * ROWS // parts)
                    nc.vector.tensor_tensor(
                        zt[:, g // 2, rows, 64 * (g % 2):64 * (g % 2 + 1)].rearrange("p r n -> p n r"),
                        ps_ab[:].rearrange("p (n r) -> p n r", r=ROWS)[:, :, rows],
                        gate[:, g % 2, :].rearrange("p (n r) -> p n r", r=ROWS)[:, :, rows],
                        ALU.mult).then_inc(zt_ready, 1)

            def x1_out(w, n):
                dve.wait_ge(o_done, 2 * w + n + 1)
                if n == 0:
                    dve.wait_ge(xb_ready, 2 * w + 2)
                rows = slice(n * ROWS // 2, (n + 1) * ROWS // 2)
                nc.vector.tensor_tensor(
                    x1[:, w, :, rows, :].rearrange("p n r d -> p r n d"),
                    ps_o[:, 512 * n:512 * n + 512].rearrange("p (r n d) -> p r n d", n=2, d=D),
                    xb[:, w, :, rows, :].rearrange("p n r d -> p r n d"), ALU.add).then_inc(x1_ready, 1)

            def x1_stats(w, n, p2):
                if p2 == 0:
                    dve.wait_ge(x1_ready, 2 * w + n + 1)
                last = nc.vector.bn_stats(
                    part[:, 1, w, p2, n, :],
                    x1[:, w, p2, n * ROWS // 2:(n + 1) * ROWS // 2, :].rearrange("p r d -> p (r d)"))
                if n == 1 and p2 == 1:
                    link(last)
                    partition_stats(1, range(w, w + 1), 2)

            def x1_mean(w):
                group_stats(X1JOB + w, 1, range(w, w + 1))
                link(nc.vector.tensor_scalar(pad[:, w, :], mean[:, 1, w, :], last_block, None, ALU.mult))
                dve.wait_ge(row_done, w + 1)
                nc.vector.tensor_tensor(
                    x1[:, w, :, ROWS, :], ps_row.rearrange("p (n d) -> p n d", d=D),
                    pad[:, w, :].rearrange("p (n o) -> p n o", o=1).broadcast_to([128, 2, D]),
                    ALU.add).then_inc(row_ready, 1)

            def x1_variance(w):
                group_variance(X1JOB + w, 1, range(w, w + 1))

            def filter_coefs(w):
                minus_mean_rstd(X1JOB + w, 1, range(w, w + 1))
                h = w % 2
                for k, cols in ((1, slice(4, 6)), (0, slice(0, 4))):
                    n = cols.stop - cols.start
                    last = nc.vector.tensor_tensor(
                        coef[:, w, :, cols], own_taps[:, h, :, cols],
                        norm[:, 1, w, k, :].rearrange("p (n o) -> p n o", o=1).broadcast_to([128, 2, n]), ALU.mult)
                link(last)
                nc.vector.tensor_scalar_add(coef[:, w, :, 0:1], coef[:, w, :, 0:1], 1.0).then_inc(coef_ready, 1)

            def filter_right(w, p2):
                dve.wait_ge(base_ready, 2 * w + p2 + 1)
                left = y[:, w, p2, :, 0:D - 1]
                nc.vector.scalar_tensor_tensor(left, x1[:, w, p2, 0:ROWS, 1:D], coef[:, w, p2, 1:2], left,
                                               ALU.mult, ALU.add).then_inc(right_ready, 1)

            def filter_below(w):
                dve.wait_ge(y_pool, 2 * w + 1)
                yw = y[:, w, 0, :, :]
                nc.vector.scalar_tensor_tensor(yw, x1[:, w, 0, 1:ROWS + 1, :], coef[:, w, 0, 2:3], yw, ALU.mult,
                                               ALU.add).then_inc(y_dve, 1)

            def edge_correction(p2):
                w = WAVES - 2
                dve.wait_ge(base_ready, 2 * w + p2 + 1)
                edge = y[:, w, p2, :, D - 1:D]
                nc.vector.tensor_scalar(edge, edge, coef[:, w, p2, 5:6], None, ALU.add).then_inc(edge_ready, 1)

            def last_tap(k):
                w, row = WAVES - 1, k // 2
                left = y[:, w, 0, :, 0:D - 1]
                link(nc.vector.scalar_tensor_tensor(left, x1[:, w, 0, row:ROWS + row, 1:D],
                                                    own_taps[:, w % 2, 0, k:k + 1], left, ALU.mult, ALU.add))

            def last_filter(p2):
                w = WAVES - 1
                yw = y[:, w, p2, :, :]
                dve.wait_ge(rstd_done, X1JOB + w + 1)
                nc.vector.scalar_tensor_tensor(yw, yw, norm[:, 1, w, 0, p2:p2 + 1], x1[:, w, p2, 0:ROWS, :],
                                               ALU.mult, ALU.add).then_inc(y_dve, 1)

            def taps_out():
                dve.wait_ge(params_in, 16)
                taps = own_taps[:].rearrange("p h n k -> p (h n) k")
                nc.vector.tensor_copy(taps[:, :, 0:4].rearrange("p n (a b) -> p n a b", b=2), ftap[:, :, 1:4:2, 1:4:2])
                nc.vector.tensor_reduce(taps[:, :, 4], ftap[:, :, 1:4:2, 1:4:2], mybir.AxisListType.XY, ALU.add)
                link(nc.vector.tensor_reduce(taps[:, :, 5], ftap[:, :, 1:4:2, 3:4], mybir.AxisListType.XY, ALU.add))
                nc.vector.tensor_scalar(taps[:, :, 5:6], taps[:, :, 5:6], -1.0, None, ALU.mult).then_inc(taps_ready, 1)
                dve.wait_ge(taps_ready, 1)

            nc.vector.memset(zeros[:], 0.0).then_inc(zeros_set, 1)
            for r in range(2):
                nc.vector.memset(abd[0:64, r, :, :, 1, :], 0.0)
                last = nc.vector.memset(abd[64:128, r, :, :, 0, :], 0.0)
            last.then_inc(abd_zeroed, 1)
            x_stats(0)
            partition_stats(0, XJOBS[0], 1)
            group_stats(0, 0, XJOBS[0])
            dve.wait_ge(masks_in, 16)
            x_shares(0)
            group_variance(0, 0, XJOBS[0])
            x_scalars(0)
            scalars_out(0)
            dve.wait_ge(stat_read, nth(0, 2))
            dve.wait_ge(t_done, 1)
            for c in DVE0:
                last = nc.vector.tensor_scalar(rt[:, 0, c * 128:c * 128 + 128], ps_ab[:, c * 128:c * 128 + 128],
                                               scalar_of(0, c, 0), scalar_of(0, c, 1), ALU.mult, ALU.add)
            last.then_inc(rt0_dve, 1)
            x_stats(1)
            partition_stats(0, XJOBS[1], 1)
            for g in range(GROUPS):
                if g == 1:
                    x_scalars(1)
                    x_stats(2, (0,))
                    scalars_out(1)
                    x_stats(2, (1,))
                elif g == 2:
                    taps_out()
                    group_stats(2, 0, XJOBS[2])
                elif g == 3:
                    scalars_out(2)
                w = g // 2 - 1
                if g >= 2 and g % 2 == 0:
                    x1_out(w, 0)
                    x1_stats(w, 0, 0)
                    x1_stats(w, 0, 1)
                elif g >= 2:
                    x1_mean(w)
                b_out(g)
                if g == 0:
                    group_stats(1, 0, XJOBS[1])
                    group_variance(1, 0, XJOBS[1])
                    x_shares(1)
                elif g == 1:
                    x_stats(3)
                    partition_stats(0, XJOBS[2], 1)
                elif g == 2:
                    group_variance(2, 0, XJOBS[2])
                    x_shares(2)
                if g >= 2 and g % 2 == 0:
                    x1_out(w, 1)
                    if g == 2:
                        x_scalars(2)
                    x1_stats(w, 1, 0)
                    x1_stats(w, 1, 1)
                elif g >= 2:
                    x1_variance(w)
                    if w >= 1:
                        filter_below(w - 1)
                    filter_coefs(w)
                if g >= 4 and g % 2 == 0:
                    filter_right(w - 1, 1)
                z_out(g, 2 if g == GROUPS - 1 else 1)
            last = WAVES - 1
            edge_correction(0)
            filter_right(last - 1, 0)
            x1_out(last, 0)
            x1_stats(last, 0, 0)
            x1_out(last, 1)
            x1_stats(last, 0, 1)
            x1_stats(last, 1, 0)
            x1_stats(last, 1, 1)
            edge_correction(1)
            dve.wait_ge(last_base, 1)
            last_tap(1)
            x1_mean(last)
            edge = y[:, last, :, :, D - 1:D]
            nc.vector.tensor_scalar(edge[:, 0, :, :], edge[:, 0, :, :], offs[:, 0, 1:2], None, ALU.add)
            x1_variance(last)
            dve.wait_ge(row_ready, WAVES)
            last_tap(3)
            dve.wait_ge(last_base, 2)
            link(nc.vector.tensor_tensor(y[:, last, 0, :, :], y[:, last, 0, :, :], last_below[:], ALU.add))
            last_filter(0)
            dve.wait_ge(last_sum_ready, 1)
            link(nc.vector.tensor_scalar(edge[:, 1, :, :], edge[:, 1, :, :], offs[:, 1, 1:2], None, ALU.add))
            last_filter(1)

        @block.tensor
        def _(pe):
            def idle_products(n):
                for _ in range(n):
                    nc.tensor.matmul(ps_g[:, 0:128], zeros[:], zeros[:], start=True, stop=True)

            def stat_product(job, step):
                pe.wait_ge(to_stat, nth(job, step))
                if nth(job, step) > 1:
                    pe.wait_ge(stat_read, nth(job, step) - 1)
                ws = XJOBS[job] if job < X1JOB else range(job - X1JOB, job - X1JOB + 1)
                k, s, n = int(job >= X1JOB), slice(ws.start, ws.stop), 2 * len(ws)
                if step < 2:
                    operand = mv[:, k, s, :, 0] if step == 0 else second[:, k, s, :]
                    nc.tensor.matmul(ps_stat[:, 0:n], average, operand, start=True, stop=True).then_inc(stat_done, 1)
                else:
                    for p2 in range(2):
                        last = nc.tensor.matmul(ps_stat[64 * p2:64 * p2 + 64, 0:n * CHUNKS], spread,
                                                sel[:, p2, s, :, :].rearrange("p w k c -> p (w k c)"),
                                                start=True, stop=True)
                    last.then_inc(stat_done, 1)

            def transposes(g):
                pe.wait_ge(nat_in[g], 16)
                if g >= 2:
                    pe.wait_ge(rt_ready, g)
                for c in range(CH):
                    p = g * GP + 2 * c
                    ps = ps_ab if g == 0 and c in DVE0 else ps_o if g == 1 else ps_t
                    last = nc.tensor.transpose(ps[:, c * 128:(c + 1) * 128],
                                               xnat[:, p:p + 2, :].rearrange("p n d -> p (n d)"), ident)
                last.then_inc(t_done, 1)

            def product_a(g):
                if g == 0:
                    pe.wait_ge(rt0_dve, 1)
                pe.wait_ge(rt_ready, g + 1)
                if g >= 1:
                    pe.wait_ge(abd_ready, g)
                nc.tensor.matmul(ps_a[:], W_A, rt[:, g, :], start=True, stop=True).then_inc(a_done, 1)

            def product_b(g):
                if g >= 1:
                    pe.wait_ge(bsb_ready, g)
                for c in range(CH):
                    last = nc.tensor.matmul(ps_b[:, c * 128:(c + 1) * 128], rt[:, g, c * 128:(c + 1) * 128], W_B,
                                            start=True, stop=True)
                last.then_inc(b_done, 1)

            def product_g(g):
                if g >= 1:
                    pe.wait_ge(gate_ready, g)
                nc.tensor.matmul(ps_g[:], W_G, rt[:, g, :], start=True, stop=True).then_inc(g_done, 1)

            def product_ab(g):
                pe.wait_ge(abd_ready, g + 1)
                pe.wait_ge(bsb_ready, g + 1)
                if g >= 1:
                    pe.wait_ge(zt_ready, g)
                for c in range(CH):
                    for p2 in range(2):
                        last = nc.tensor.matmul(
                            ps_ab[64 * p2:64 * p2 + 64, c * 128:(c + 1) * 128],
                            bsb[:, g % 2, c, 64 * p2:64 * p2 + 64],
                            abd[:, g % 2, c, p2, :, :].rearrange("p t j -> p (t j)"), start=True, stop=True)
                last.then_inc(ab_done, 1)

            def product_o(w, n):
                pe.wait_ge(zt_ready, 2 * w + 2 + (n if w == WAVES - 1 else 0))
                if w >= 1:
                    pe.wait_ge(row_ready, w)
                for r in range(n * ROWS // 2, (n + 1) * ROWS // 2):
                    last = nc.tensor.matmul(ps_o[:, r * 128:(r + 1) * 128],
                                            zt[:, w, r, :], W_O, start=True, stop=True)
                last.then_inc(o_done, 1)

            def rows_below(w):
                pe.wait_ge(x1_ready, 2 * w + 2)
                nc.tensor.matmul(ps_row, above, x1[:, w, :, 0, :], start=True, stop=True).then_inc(row_done, 1)

            def last_sum(k, rows):
                w, row, col = WAVES - 1, k // 2, k % 2
                n = rows.stop - rows.start
                out_rows = ps_a[:].rearrange("p (r d) -> p r d", d=D)[:, rows.start:rows.stop, 0:D - col]
                in_rows = x1[:, w, 1, rows.start + row:rows.stop + row, col:D]
                return nc.tensor.matmul(out_rows, diag[:, k, :], in_rows, start=(k == 0),
                                        stop=(k == 3 and rows.stop == ROWS))

            pe.wait_ge(zeros_set, 1)
            idle_products(IDLE[0])
            pe.wait_ge(masks_in, 16)
            stat_product(0, 0)
            idle_products(IDLE[1])
            stat_product(0, 1)
            transposes(0)
            transposes(1)
            idle_products(IDLE[2])
            stat_product(0, 2)
            idle_products(IDLE[3])
            pe.wait_ge(params_in, 16)
            for g in range(GROUPS):
                w = g // 2 - 1
                product_a(g)
                if 1 <= g < GROUPS - 1:
                    transposes(g + 1)
                if g == 1:
                    stat_product(1, 2)
                elif g == 2:
                    stat_product(2, 0)
                elif g == 3:
                    stat_product(2, 2)
                if g >= 2 and g % 2 == 0:
                    product_o(w, 0)
                elif g >= 2:
                    rows_below(w)
                    stat_product(X1JOB + w, 0)
                product_b(g)
                if g == 0:
                    stat_product(1, 0)
                elif g == 2:
                    stat_product(2, 1)
                if g >= 2 and g % 2 == 0:
                    product_o(w, 1)
                elif g >= 2:
                    stat_product(X1JOB + w, 1)
                product_g(g)
                product_ab(g)
                if g == 0:
                    stat_product(1, 1)
            last = WAVES - 1
            for n in range(2):
                product_o(last, n)
            rows_below(last)
            pe.wait_ge(diag_ready, 1)
            pe.wait_ge(abd_ready, GROUPS)
            last_sum(0, range(0, ROWS))
            stat_product(X1JOB + last, 0)
            last_sum(1, range(0, ROWS))
            last_sum(2, range(0, ROWS - 1))
            stat_product(X1JOB + last, 1)
            last_sum(3, range(0, ROWS - 1))
            pe.wait_ge(row_ready, WAVES)
            last_sum(2, range(ROWS - 1, ROWS))
            last_sum(3, range(ROWS - 1, ROWS)).then_inc(sum_pe, 1)


def kernel(x, L0_conv_Wa, L0_conv_ba, L0_conv_Wb, L0_conv_bb, L0_conv_Wg, L0_conv_bg, L0_conv_Wo, L0_conv_bo,
           L1_conv_filt):
    import concourse.bacc as _bacc
    from concourse.bass_utils import run_bass_kernel_spmd as _run

    given = [np.asarray(a) for a in (L0_conv_Wa, L0_conv_ba, L0_conv_Wb, L0_conv_bb, L0_conv_Wg, L0_conv_bg,
                                     L0_conv_Wo, L0_conv_bo, L1_conv_filt)]
    arrays = {
        "x": np.ascontiguousarray(x),
        "params": np.ascontiguousarray(np.concatenate(mask_columns() + parameter_columns(*given), axis=1)),
    }
    nc = _bacc.Bacc("TRN2", target_bir_lowering=False, num_devices=1)
    args = [nc.dram_tensor(n, a.shape, mybir.dt.from_np(a.dtype), kind="ExternalInput").ap()
            for n, a in arrays.items()]
    out = nc.dram_tensor("out", arrays["x"].shape, mybir.dt.float32, kind="ExternalOutput").ap()
    preact_pair_mix_blur(nc, *args, out)
    return _run(nc, [arrays], core_ids=[0]).results[0]["out"]
```
